# Optimizing a Trainium2 kernel written in Bass

```python
import numpy as np
import jax
import jax.numpy as jnp

def _softmax(x, axis=-1):
    return jax.nn.softmax(x, axis=axis)

def _gelu(x):
    return jax.nn.gelu(x, approximate=True)

def _silu(x):
    return jax.nn.silu(x)

def _sigmoid(x):
    return jax.nn.sigmoid(x)

def _layernorm(x, axis=-1, eps=1e-05):
    m = jnp.mean(x, axis=axis, keepdims=True)
    v = jnp.var(x, axis=axis, keepdims=True)
    return (x - m) / jnp.sqrt(v + eps)

def _scatter_add(tgt, idx, src, axis=0):
    return tgt.at[idx].add(src)

def _segment_sum(src, seg, n):
    return jax.ops.segment_sum(src, seg, n)
kernel_name = 'mk_cond_resid_d4_seqx_r4_d24747'

def setup_inputs(seed: int=0):
    np.random.seed(seed)
    _w = jnp.asarray

    def _rec_inputs():
        import jax
        import jax.numpy as jnp
        _rk = jax.random.key(seed)
        x = 7.22e-05 + 1 * jax.random.normal(jax.random.fold_in(_rk, 1), (4, 512, 512), jnp.float32)
        _lenS = 512 - jax.random.randint(jax.random.fold_in(_rk, 7), (4,), 0, max(1, 512 // 4) + 1, jnp.int32)
        _lenS2 = 512 - jax.random.randint(jax.random.fold_in(_rk, 8), (4,), 0, max(1, 512 // 4) + 1, jnp.int32)
        cond_2048 = 0.0061147 + 1.02565 * jax.random.normal(jax.random.fold_in(_rk, 11), (4, 512), jnp.float32)
        fside_BxSx1_0 = -0.00499425 + 1.0058 * jax.random.normal(jax.random.fold_in(_rk, 12), (4, 512, 1), jnp.float32)
        return (x, cond_2048, fside_BxSx1_0)
    x, cond_2048, fside_BxSx1_0 = _rec_inputs()

    def _L0_cond_setup():
        import jax, jax.numpy as jnp
        import numpy as np
        DIM = 512
        H = 16
        DH = 128
        INNER = H * DH
        MLP = 4 * DIM
        B, T = (2, 512)
        EPS = 1e-06

        def _ln(x):
            mu = jnp.mean(x, axis=-1, keepdims=True)
            var = jnp.var(x, axis=-1, keepdims=True)
            return (x - mu) * jax.lax.rsqrt(var + EPS)
        key = jax.random.key(seed)
        ks = jax.random.split(key, 12)
        s = 0.02
        return {'x': jax.random.normal(ks[0], (B, T, DIM), jnp.float32), 'timestep_embed': jax.random.normal(ks[1], (B, DIM), jnp.float32), 'ada_w': jax.random.normal(ks[2], (DIM, 6 * DIM), jnp.float32) * s, 'ada_b': jnp.zeros((6 * DIM,), jnp.float32), 'qkv_w': jax.random.normal(ks[3], (DIM, 3 * INNER), jnp.float32) * s, 'qkv_b': jnp.zeros((3 * INNER,), jnp.float32), 'out_w': jax.random.normal(ks[4], (INNER, DIM), jnp.float32) * s, 'out_b': jnp.zeros((DIM,), jnp.float32), 'ffn_w1': jax.random.normal(ks[5], (DIM, MLP), jnp.float32) * s, 'ffn_b1': jnp.zeros((MLP,), jnp.float32), 'ffn_w2': jax.random.normal(ks[6], (MLP, DIM), jnp.float32) * s, 'ffn_b2': jnp.zeros((DIM,), jnp.float32)}
    _L0_cond_all = _L0_cond_setup()
    _L0_cond_in = {k: v for k, v in _L0_cond_all.items() if k in ('ada_w', 'ada_b', 'qkv_w', 'qkv_b', 'out_w', 'out_b', 'ffn_w1', 'ffn_b1', 'ffn_w2', 'ffn_b2')}
    del _L0_cond_all

    def _L1_cond_setup():
        import jax, jax.numpy as jnp
        import numpy as np
        key = jax.random.key(seed)
        k1, k2, k3 = jax.random.split(key, 3)
        B, L, D, K = (4, 1024, 512, 4)
        x = jax.random.normal(k1, (B, L, D), dtype=jnp.float32)
        w = jax.random.normal(k2, (K, 1, D), dtype=jnp.float32) * 0.1
        b = jax.random.normal(k3, (D,), dtype=jnp.float32) * 0.1
        return {'x': x, 'w': w, 'b': b}
    _L1_cond_all = _L1_cond_setup()
    _L1_cond_in = {k: v for k, v in _L1_cond_all.items() if k in ('b',)}
    del _L1_cond_all

    def _L2_cond_setup():
        import jax, jax.numpy as jnp
        import numpy as np
        DT = 0.01
        EPSILON = 0.08
        ALPHA = 0.7
        BETA = 0.8
        CLAMP = 20.0
        B, T, N = (64, 128, 512)

        def _derivative(q, p, drive, coupling, bias):
            i_couple = jnp.tanh(q) @ coupling.T
            dq = q - q ** 3 / 3.0 - p + drive + i_couple + bias
            dp = EPSILON * (q + ALPHA - BETA * p)
            return (dq, dp)

        def _rk4_step(q, p, drive, coupling, bias):
            dq1, dp1 = _derivative(q, p, drive, coupling, bias)
            dq2, dp2 = _derivative(q + 0.5 * DT * dq1, p + 0.5 * DT * dp1, drive, coupling, bias)
            dq3, dp3 = _derivative(q + 0.5 * DT * dq2, p + 0.5 * DT * dp2, drive, coupling, bias)
            dq4, dp4 = _derivative(q + DT * dq3, p + DT * dp3, drive, coupling, bias)
            q_next = q + DT / 6.0 * (dq1 + 2 * dq2 + 2 * dq3 + dq4)
            p_next = p + DT / 6.0 * (dp1 + 2 * dp2 + 2 * dp3 + dp4)
            q_next = jnp.clip(q_next, -CLAMP, CLAMP)
            p_next = jnp.clip(p_next, -CLAMP, CLAMP)
            return (q_next, p_next)
        key = jax.random.key(seed)
        k1, k2, k3, k4 = jax.random.split(key, 4)
        return {'q0': jax.random.normal(k1, (B, N), dtype=jnp.float32), 'p0': jax.random.normal(k2, (B, N), dtype=jnp.float32), 'input_drive_seq': jax.random.normal(k3, (B, T, N), dtype=jnp.float32), 'coupling': jax.random.normal(k4, (N, N), dtype=jnp.float32) * 0.01, 'bias': jnp.zeros((N,), dtype=jnp.float32)}
    _L2_cond_all = _L2_cond_setup()
    _L2_cond_in = {k: v for k, v in _L2_cond_all.items() if k in ('coupling', 'bias')}
    del _L2_cond_all

    def _L3_cond_setup():
        import jax, jax.numpy as jnp
        import numpy as np
        G, N, K = (16, 512, 5120)
        key = jax.random.key(seed)
        k1, k2, k3 = jax.random.split(key, 3)
        return {'emb_s': jax.random.normal(k1, (G, N, 1), dtype=jnp.float32), 'emb_t': jax.random.normal(k2, (G, 1, N), dtype=jnp.float32), 'attention_weights': jax.random.normal(k3, (G, N, N), dtype=jnp.float32), 'k': K}
    _L3_cond_all = _L3_cond_setup()
    _L3_cond_in = {k: v for k, v in _L3_cond_all.items() if k in ()}
    del _L3_cond_all
    return {'x': x, 'cond_2048': cond_2048, 'fside_BxSx1_0': fside_BxSx1_0, 'L0_cond_ada_w': _L0_cond_in['ada_w'], 'L0_cond_ada_b': _L0_cond_in['ada_b'], 'L0_cond_qkv_w': _L0_cond_in['qkv_w'], 'L0_cond_qkv_b': _L0_cond_in['qkv_b'], 'L0_cond_out_w': _L0_cond_in['out_w'], 'L0_cond_out_b': _L0_cond_in['out_b'], 'L0_cond_ffn_w1': _L0_cond_in['ffn_w1'], 'L0_cond_ffn_b1': _L0_cond_in['ffn_b1'], 'L0_cond_ffn_w2': _L0_cond_in['ffn_w2'], 'L0_cond_ffn_b2': _L0_cond_in['ffn_b2'], 'L1_cond_b': _L1_cond_in['b'], 'L2_cond_coupling': _L2_cond_in['coupling'], 'L2_cond_bias': _L2_cond_in['bias']}

def reference(x, cond_2048, fside_BxSx1_0, L0_cond_ada_w, L0_cond_ada_b, L0_cond_qkv_w, L0_cond_qkv_b, L0_cond_out_w, L0_cond_out_b, L0_cond_ffn_w1, L0_cond_ffn_b1, L0_cond_ffn_w2, L0_cond_ffn_b2, L1_cond_b, L2_cond_coupling, L2_cond_bias):
    import jax
    import jax.numpy as jnp

    def _L0_cond_ref(x, timestep_embed, ada_w, ada_b, qkv_w, qkv_b, out_w, out_b, ffn_w1, ffn_b1, ffn_w2, ffn_b2):
        import jax, jax.numpy as jnp
        import numpy as np
        DIM = 512
        H = 16
        DH = 128
        INNER = H * DH
        MLP = 4 * DIM
        B, T = (2, 512)
        EPS = 1e-06

        def _ln(x):
            mu = jnp.mean(x, axis=-1, keepdims=True)
            var = jnp.var(x, axis=-1, keepdims=True)
            return (x - mu) * jax.lax.rsqrt(var + EPS)
        Bc, Tc, D = x.shape
        ada = (timestep_embed @ ada_w + ada_b)[:, None, :]
        shift1, scale1, gate1, shift2, scale2, gate2 = jnp.split(ada, 6, axis=-1)
        x1 = _ln(x) * (1.0 + scale1) + shift1
        qkv = (x1 @ qkv_w + qkv_b).reshape(Bc, Tc, 3, H, DH)
        q, k, v = (qkv[:, :, 0], qkv[:, :, 1], qkv[:, :, 2])
        scale = DH ** (-0.5)
        attn = jnp.einsum('bthd,bshd->bhts', q, k) * scale
        attn = jax.nn.softmax(attn, axis=-1)
        attn_out = jnp.einsum('bhts,bshd->bthd', attn, v).reshape(Bc, Tc, INNER)
        attn_out = attn_out @ out_w + out_b
        x = x + gate1 * attn_out
        x2 = _ln(x) * (1.0 + scale2) + shift2
        h = jax.nn.gelu(x2 @ ffn_w1 + ffn_b1, approximate=False)
        x = x + gate2 * (h @ ffn_w2 + ffn_b2)
        return x

    def _L1_cond_ref(x, w, b):
        import jax, jax.numpy as jnp
        import numpy as np
        'Depthwise causal conv1d, channel-last.\n            x: (B, L, D); w: (K, 1, D); b: (D,). Returns (B, L, D).\n            Matches torch: Conv1d(D, D, K, groups=D, padding=K-1)(x.T)[..., :L].T\n            which is exactly a causal conv (left pad K-1, trim to L).\n            '
        K = w.shape[0]
        D = x.shape[-1]
        y = jax.lax.conv_general_dilated(x, w, window_strides=(1,), padding=[(K - 1, 0)], feature_group_count=D, dimension_numbers=('NWC', 'WIO', 'NWC'))
        return y + b

    def _L2_cond_ref(q0, p0, input_drive_seq, coupling, bias):
        import jax, jax.numpy as jnp
        import numpy as np
        DT = 0.01
        EPSILON = 0.08
        ALPHA = 0.7
        BETA = 0.8
        CLAMP = 20.0
        B, T, N = (64, 128, 512)

        def _derivative(q, p, drive, coupling, bias):
            i_couple = jnp.tanh(q) @ coupling.T
            dq = q - q ** 3 / 3.0 - p + drive + i_couple + bias
            dp = EPSILON * (q + ALPHA - BETA * p)
            return (dq, dp)

        def _rk4_step(q, p, drive, coupling, bias):
            dq1, dp1 = _derivative(q, p, drive, coupling, bias)
            dq2, dp2 = _derivative(q + 0.5 * DT * dq1, p + 0.5 * DT * dp1, drive, coupling, bias)
            dq3, dp3 = _derivative(q + 0.5 * DT * dq2, p + 0.5 * DT * dp2, drive, coupling, bias)
            dq4, dp4 = _derivative(q + DT * dq3, p + DT * dp3, drive, coupling, bias)
            q_next = q + DT / 6.0 * (dq1 + 2 * dq2 + 2 * dq3 + dq4)
            p_next = p + DT / 6.0 * (dp1 + 2 * dp2 + 2 * dp3 + dp4)
            q_next = jnp.clip(q_next, -CLAMP, CLAMP)
            p_next = jnp.clip(p_next, -CLAMP, CLAMP)
            return (q_next, p_next)
        drive_tbn = jnp.swapaxes(input_drive_seq, 0, 1)

        def scan_fn(carry, drive):
            q, p = carry
            q, p = _rk4_step(q, p, drive, coupling, bias)
            return ((q, p), q)
        (_, _), q_trace_tbn = jax.lax.scan(scan_fn, (q0, p0), drive_tbn)
        return jnp.swapaxes(q_trace_tbn, 0, 1)

    def _L3_cond_ref(emb_s, emb_t, attention_weights, k):
        import jax, jax.numpy as jnp
        import numpy as np
        G, N, K = (16, 512, 5120)
        g, n = (emb_s.shape[0], emb_s.shape[1])
        adj = emb_s * emb_t
        att = jax.nn.softmax(attention_weights, axis=-1) * (1.0 / np.sqrt(n).astype(np.float32))
        adj = adj * att
        diag = jnp.arange(n)
        adj = adj.at[:, diag, diag].set(-jnp.inf)
        flat = adj.reshape(g, n * n)
        _, idx = jax.lax.top_k(flat, k)
        rows = jnp.arange(g)[:, None]
        out = jnp.zeros((g, n * n), dtype=adj.dtype).at[rows, idx].set(1.0)
        return out.reshape(g, n, n)
    x = x + _L0_cond_ref(x, cond_2048, L0_cond_ada_w, L0_cond_ada_b, L0_cond_qkv_w, L0_cond_qkv_b, L0_cond_out_w, L0_cond_out_b, L0_cond_ffn_w1, L0_cond_ffn_b1, L0_cond_ffn_w2, L0_cond_ffn_b2)
    x = x + _L1_cond_ref(x, cond_2048[:, None, :], L1_cond_b)
    x = x + _L2_cond_ref(cond_2048, cond_2048, x, L2_cond_coupling, L2_cond_bias)
    x = x + _L3_cond_ref(fside_BxSx1_0, cond_2048[:, None, :], x, 5120)
    return x

_drawn_inputs = setup_inputs


def setup_inputs(seed=0):
    import zlib

    import numpy as np

    out = dict(_drawn_inputs(seed))
    spreads = {'L0_cond_ada_b': (0.0, 0.1),
     'L0_cond_qkv_b': (0.0, 0.1),
     'L0_cond_out_b': (0.0, 0.1),
     'L0_cond_ffn_b1': (0.0, 0.1),
     'L0_cond_ffn_b2': (0.0, 0.1),
     'L2_cond_bias': (0.0, 0.1)}
    factors = {}
    for name, (base, spread) in spreads.items():
        noise = np.random.default_rng([zlib.crc32(name.encode()), seed]).standard_normal(out[name].shape)
        drawn = base * np.exp(spread * noise) if base else spread * noise
        out[name] = jnp.asarray(drawn.astype(out[name].dtype))
    for name, factor in factors.items():
        out[name] = (out[name] * factor).astype(out[name].dtype)
    return out
```

```python
import concourse.bass as bass
from concourse import mybir
from contextlib import ExitStack

F32 = mybir.dt.float32
I32 = mybir.dt.int32
BF16 = mybir.dt.bfloat16
ACT = mybir.ActivationFunctionType
ALU = mybir.AluOpType
AX = mybir.AxisListType

P = 128
B, T, D = 4, 512, 512
TC, DC = T // P, D // P
NTILE = B * TC
HEADS, DH = 16, 128
INNER = HEADS * DH
MLP = 2048
MC = MLP // P
QSCALE = DH ** -0.5
LN_EPS = 1e-6
TOPK = 5120
H_STEP, EPSILON, ALPHA, BETA, CLAMP = 0.01, 0.08, 0.7, 0.8, 20.0
P_SHIFT = ALPHA / BETA
KEEP_WARM = 8


VECS = MC + NTILE + 2 * DC + 3 * HEADS


class Memory:

    def __init__(self, nc, ctx):
        def sb(name, shape, dt=F32):
            return ctx.enter_context(nc.sbuf_tensor(name, shape, dt))

        self.tok = sb("tok", [P, NTILE, D])
        self.acc = sb("acc", [P, NTILE, D])
        self.feat = sb("feat", [P, DC, B, T])
        self.gate = sb("gate", [P, 2, B, D])
        self.work = sb("work", [P, 22400])
        self.ident = sb("ident", [P, P])
        self.sel = sb("sel", [B, B, P])
        self.condT = sb("condT", [P, DC, B])
        self.adaT = sb("adaT", [P, 4, DC, B])
        self.out_b = sb("out_b", [P, D])
        self.b2 = sb("b2", [P, D])
        self.vecT = sb("vecT", [P, VECS])
        self.b1T = self.vecT[:, 0:MC]
        self.emb_s = self.vecT[:, MC:MC + NTILE]
        self.convbT = self.vecT[:, 32:32 + DC]
        self.cbiasT = self.vecT[:, 36:36 + DC]
        self.qkv_bT = self.vecT[:, 40:40 + 3 * HEADS].rearrange("p (t h) -> p t h", t=3)
        self.stats = sb("stats", [P, NTILE, 6])
        self.mv = sb("mv", [P, NTILE, 2])
        self.rstd = sb("rstd", [P, 2, NTILE])
        self.small = sb("small", [P, 64])
        self.psum = [ctx.enter_context(nc.psum_tensor(f"bank{i}", [P, 512], F32)) for i in range(8)]
        self.const_ready = ctx.enter_context(nc.semaphore("const_ready"))
        self.vec_loaded = ctx.enter_context(nc.semaphore("vec_loaded"))
        self.vecT_ready = ctx.enter_context(nc.semaphore("vecT_ready"))
        self.w1_loaded = ctx.enter_context(nc.semaphore("w1_loaded"))
        self.coupling_loaded = ctx.enter_context(nc.semaphore("coupling_loaded"))

    def cut(self, start, shape):
        n = 1
        for s in shape:
            n *= s
        flat = self.work[:, start:start + n]
        if len(shape) == 1:
            return flat
        names = "abc"[:len(shape)]
        return flat.rearrange(f"p ({' '.join(names)}) -> p {' '.join(names)}",
                              **{k: v for k, v in zip(names, shape)})


def layernorm_engines(nc, ctx, mem, block_name, src, shift, norm, cond_ready):
    def sem(name):
        return ctx.enter_context(nc.semaphore(f"{block_name}_{name}"))

    stat, var_ready, std_ready, norm_ready, turned, act_out, dve_out = (
        sem(n) for n in ("stat", "var_ready", "std_ready", "norm_ready", "turned", "act_out", "dve_out"))
    bank = mem.psum[4:8]

    def dve(e, src_ready):
        for b in range(B):
            src_ready(e, b)
            tiles = range(b * TC, (b + 1) * TC)
            for t in tiles:
                e.bn_stats(mem.stats[:, t], src[:, t]).then_inc(stat, 1)
            for n, t in enumerate(tiles):
                e.wait_ge(stat, (2 * b) * TC + n + 1)
                e.bn_aggr(mem.mv[:, t], mem.stats[:, t]).then_inc(stat, 1)
            e.wait_ge(stat, (2 * b + 2) * TC)
            e.tensor_scalar(mem.rstd[:, 0, b * TC:(b + 1) * TC], mem.mv[:, b * TC:(b + 1) * TC, 1],
                            LN_EPS, None, ALU.add).then_inc(var_ready, 1)
            e.wait_ge(std_ready, 2 * b + 1)
            e.reciprocal(mem.rstd[:, 1, b * TC:(b + 1) * TC],
                         mem.rstd[:, 0, b * TC:(b + 1) * TC]).then_inc(std_ready, 1)
            e.wait_ge(std_ready, 2 * b + 2)
            if b >= 2:
                e.wait_ge(turned, DC * (b - 1))
            for n, t in enumerate(tiles):
                e.tensor_scalar(norm[:, b % 2, n], src[:, t], mem.mv[:, t, 0:1],
                                mem.rstd[:, 1, t:t + 1], ALU.subtract, ALU.mult).then_inc(norm_ready, 1)
            cond_ready(e)
            for c in (1, 3):
                e.wait_ge(turned, DC * b + c + 1)
                e.tensor_scalar(mem.feat[:, c, b], bank[c][:, :], mem.adaT[:, shift + 1, c, b:b + 1],
                                mem.adaT[:, shift, c, b:b + 1], ALU.mult, ALU.add).then_inc(dve_out, 1)

    def act(e):
        for b in range(B):
            e.wait_ge(var_ready, b + 1)
            e.activation(mem.rstd[:, 0, b * TC:(b + 1) * TC], mem.rstd[:, 0, b * TC:(b + 1) * TC],
                         ACT.Sqrt).then_inc(std_ready, 1)
            cond_ready(e)
            for c in (0, 2):
                e.wait_ge(turned, DC * b + c + 1)
                e.activation(mem.feat[:, c, b], bank[c][:, :], ACT.Identity,
                             bias=mem.adaT[:, shift, c, b:b + 1],
                             scale=mem.adaT[:, shift + 1, c, b:b + 1]).then_inc(act_out, 1)

    def pe(e):
        for b in range(B):
            e.wait_ge(norm_ready, TC * (b + 1))
            for c in range(DC):
                if b >= 1:
                    e.wait_ge(act_out if c % 2 == 0 else dve_out, 2 * (b - 1) + c // 2 + 1)
                for n in range(TC):
                    last = e.transpose(bank[c][:, n * P:(n + 1) * P], norm[:, b % 2, n, c * P:(c + 1) * P],
                                       mem.ident[:, :])
                last.then_inc(turned, 1)

    return dve, act, pe, turned, act_out, dve_out


def prepare(nc, mem, a):
    ada_w = mem.cut(0, [DC, 6 * D])
    ada = mem.cut(12288, [6 * D])[0:B]
    norm = mem.work[:, 15360:15360 + 2 * TC * D].rearrange("p (r t d) -> p r t d", r=2, t=TC)
    rows = mem.gate[0:B].rearrange("p k b d -> p (k b d)")
    ada_b, cond = rows[:, 0:6 * D], rows[:, 6 * D:7 * D]
    vec_rows = mem.cut(19456, [P])[0:VECS]
    with ExitStack() as ctx:
        def sem(name):
            return ctx.enter_context(nc.semaphore(name))

        x_loaded = [sem(f"x_loaded{b}") for b in range(B)]
        w_loaded = [sem(f"ada_w_loaded{n}") for n in range(6)]
        cond_loaded, adab_loaded, zeroed = sem("cond_loaded"), sem("adab_loaded"), sem("zeroed")
        rows_loaded, rows_turned = sem("rows_loaded"), sem("rows_turned")
        cond_turned, condT_ready = sem("cond_turned"), sem("condT_ready")
        ada_done, ada_ready, ada_turned, adaT_ready = (sem(n) for n in ("ada_done", "ada_ready", "ada_turned", "adaT_ready"))
        gate_done, gate_ready = sem("gate_done"), sem("gate_ready")
        turned_bank, bank = mem.psum[2], mem.psum
        PARTS = (0, 1, 3, 4)

        def cond_ready(e):
            e.wait_ge(adaT_ready, 4)

        ln_dve, ln_act, ln_pe, *_ = layernorm_engines(nc, ctx, mem, "ln1", mem.tok, 0, norm, cond_ready)
        block = ctx.enter_context(nc.Block())

        @block.sync
        def _(e):
            e.dma_start(cond, a["cond"]).then_inc(cond_loaded, 16)
            e.dma_start(ada_b, a["ada_b"].rearrange("(o n) -> o n", o=1).broadcast_to((B, 6 * D))).then_inc(adab_loaded, 16)
            at = 0
            for name in ("ffn_b1", "fside", "conv_b", "bias", "qkv_b"):
                v = a[name].rearrange("b t o -> (b t o)") if name == "fside" else a[name]
                n = v.shape[0] // P
                e.dma_start(vec_rows[at:at + n], v.rearrange("(c p) -> c p", p=P)).then_inc(rows_loaded, 16)
                at += n
            w = a["ada_w"].rearrange("(c p) n -> p c n", p=P)
            x = a["x"].rearrange("b (t p) d -> b p t d", p=P)
            for n in range(6):
                if n < B:
                    e.dma_start(mem.tok[:, n * TC:(n + 1) * TC], x[n]).then_inc(x_loaded[n], 16)
                e.dma_start(ada_w[:, :, n * D:(n + 1) * D], w[:, :, n * D:(n + 1) * D]).then_inc(w_loaded[n], 16)

        @block.gpsimd
        def _(e):
            e.memset(mem.ident[:, :], 0.0).then_inc(zeroed, 1)
            e.memset(mem.sel[:, :, :], 0.0).then_inc(zeroed, 1)
            e.wait_ge(zeroed, 2)
            e.affine_select(out=mem.ident[:, :], in_=mem.ident[:, :], compare_op=ALU.not_equal, fill=1.0,
                            base=0, pattern=[[-1, P]], channel_multiplier=1).then_inc(mem.const_ready, 1)
            e.affine_select(out=mem.sel[:, :, :], in_=mem.sel[:, :, :], compare_op=ALU.not_equal, fill=1.0,
                            base=0, pattern=[[-1, B], [0, P]], channel_multiplier=1).then_inc(mem.const_ready, 1)

        @block.scalar
        def _(e):
            row = "(o n) -> o n"
            e.dma_start(mem.out_b[:, :], a["out_b"].rearrange(row, o=1).broadcast_to((P, D))).then_inc(mem.vec_loaded, 16)
            e.dma_start(mem.b2[:, :], a["ffn_b2"].rearrange(row, o=1).broadcast_to((P, D))).then_inc(mem.vec_loaded, 16)
            ln_act(e)
            for k in range(2):
                for b in range(B):
                    e.wait_ge(gate_done, k * B + b + 1)
                    e.activation(mem.gate[:, k, b], bank[b % 2][:, :], ACT.Copy).then_inc(gate_ready, 1)

        @block.tensor
        def _(e):
            e.wait_ge(mem.const_ready, 2)
            e.wait_ge(cond_loaded, 16)
            for c in range(DC):
                last = e.transpose(turned_bank[:, c * B:(c + 1) * B], cond[:, c * P:(c + 1) * P], mem.ident[0:B, 0:B])
            last.then_inc(cond_turned, 1)
            e.wait_ge(rows_loaded, 80)
            e.transpose(bank[3][:, 256:256 + VECS], vec_rows, mem.ident[0:VECS, 0:VECS]).then_inc(rows_turned, 1)
            e.wait_ge(condT_ready, 1)
            for n in range(6):
                e.wait_ge(w_loaded[n], 16)
                if n >= 2:
                    e.wait_ge(ada_ready, n - 1)
                for c in range(DC):
                    last = e.matmul(bank[n % 2][0:B, :], mem.condT[:, c], ada_w[:, c, n * D:(n + 1) * D],
                                    start=(c == 0), stop=(c == DC - 1))
                last.then_inc(ada_done, 1)
            e.wait_ge(ada_ready, 6)
            for i, part in enumerate(PARTS):
                for c in range(DC):
                    at = part * D + c * P
                    last = e.transpose(bank[3][:, (i * DC + c) * B:(i * DC + c + 1) * B], ada[:, at:at + P],
                                       mem.ident[0:B, 0:B])
            last.then_inc(ada_turned, 1)
            ln_pe(e)
            for k, part in enumerate((2, 5)):
                for b in range(B):
                    if k * B + b >= 2:
                        e.wait_ge(gate_ready, k * B + b - 1)
                    e.matmul(bank[b % 2][:, :], mem.sel[:, b, :], ada[:, part * D:(part + 1) * D],
                             start=True, stop=True).then_inc(gate_done, 1)

        @block.vector
        def _(e):
            e.wait_ge(cond_turned, 1)
            e.tensor_copy(mem.condT[:, :, :].rearrange("p c b -> p (c b)"), turned_bank[:, 0:DC * B]).then_inc(condT_ready, 1)
            e.wait_ge(rows_turned, 1)
            e.tensor_copy(mem.vecT[:, :], bank[3][:, 256:256 + VECS]).then_inc(mem.vecT_ready, 1)
            e.wait_ge(adab_loaded, 16)
            for n in range(6):
                e.wait_ge(ada_done, n + 1)
                e.tensor_tensor(ada[:, n * D:(n + 1) * D], bank[n % 2][0:B, :], ada_b[:, n * D:(n + 1) * D],
                                ALU.add).then_inc(ada_ready, 1)
            e.wait_ge(ada_turned, 1)
            for i in range(4):
                part = bank[3][:, i * DC * B:(i + 1) * DC * B]
                e.tensor_scalar(mem.adaT[:, i].rearrange("p c b -> p (c b)"), part, float(i % 2), None,
                                ALU.add).then_inc(adaT_ready, 1)
            ln_dve(e, lambda e, b: e.wait_ge(x_loaded[b], 16))


def attention(nc, mem, a):
    UNITS = 2 * B
    w = [mem.cut(i * 2048, [1536]).rearrange("p (k t d) -> p k t d", k=DC, t=3) for i in range(2)]
    out_w = [mem.cut(1536 + i * 2048, [D]) for i in range(2)]
    qkvT = mem.cut(4104, [3, T])
    probs = mem.cut(5640, [TC, T])
    probsT = mem.cut(7688, [TC, T])
    v = mem.cut(9736, [TC, DH])
    oT = mem.cut(10248, [T])
    pair_bias = mem.small[:, 16:22].rearrange("p (t i) -> p t i", t=3)
    nmax, rsum, rinv = mem.small[:, 0:TC], mem.small[:, 4:4 + TC], mem.small[:, 8:8 + TC]
    with ExitStack() as ctx:
        def sem(name):
            return ctx.enter_context(nc.semaphore(name))

        w_loaded = [sem(f"head_loaded{i}") for i in range(2)]
        acc_set, acc_done = sem("acc_set"), sem("acc_done")
        qkv_done, qkv_ready = sem("qkv_done"), sem("qkv_ready")
        score_done, max_ready, exp_ready, inv_ready, probs_ready = (
            sem(n) for n in ("score_done", "max_ready", "exp_ready", "inv_ready", "probs_ready"))
        v_turned, v_ready, p_turned, pT_ready = (sem(n) for n in ("v_turned", "v_ready", "p_turned", "pT_ready"))
        bias_ready = sem("bias_ready")
        o_done, oT_ready, proj_done = sem("o_done"), sem("oT_ready"), sem("proj_done")
        bank_qkv, bank_s, bank_t, bank_o = mem.psum[0:2], mem.psum[2:4], mem.psum[4:6], mem.psum[6:8]
        block = ctx.enter_context(nc.Block())
        PAIRS = HEADS // 2

        def bias_of(i, t):
            return pair_bias[:, t, i:i + 1]

        @block.sync
        def _(e):
            e.dma_start(mem.cut(13952, [DC, MLP]), a["ffn_w1"].rearrange("(c p) n -> p c n", p=P)).then_inc(mem.w1_loaded, 16)
            wq = a["qkv_w"].rearrange("(k p) (t h d) -> h p k t d", p=P, t=3, h=HEADS)
            wo = a["out_w"].rearrange("(h d) n -> h d n", h=HEADS)

            def load(i, head):
                for t in range(3):
                    e.dma_start(w[i][:, :, t], wq[head][:, :, t]).then_inc(w_loaded[i], 16)
                e.dma_start(out_w[i], wo[head]).then_inc(w_loaded[i], 16)

            for i in range(2):
                load(i, i)
            with e.Fori(0, PAIRS - 1) as g:
                for i in range(2):
                    e.wait_ge(acc_done, (UNITS * g + B * (i + 1)) * TC)
                    load(i, 2 * g + 2 + i)

        def pe_pair(e, g):
            def project_qkv(u):
                i, b, n = u // B, u % B, 3 * u
                if b == 0:
                    e.wait_ge(w_loaded[i], 64 * (g + 1))
                for t in range(3):
                    m = n + t
                    if isinstance(g, int) and g == 0 and m < 2:
                        pass
                    else:
                        e.wait_ge(qkv_ready, 3 * UNITS * g + m - 1)
                    for c in range(DC):
                        last = e.matmul(bank_qkv[m % 2][:, :], w[i][:, c, t], mem.feat[:, c, b],
                                        start=(c == 0), stop=(c == DC - 1))
                    last.then_inc(qkv_done, 1)

            for u in range(UNITS):
                i, b = u // B, u % B
                first = isinstance(g, int) and g == 0 and u == 0
                U = UNITS * g + u
                if u == 0:
                    project_qkv(0)
                e.wait_ge(qkv_ready, 3 * U + 3)
                for t in range(TC):
                    if not (first and t < 2):
                        e.wait_ge(exp_ready, TC * U + t - 1)
                    e.matmul(bank_s[t % 2][:, :], qkvT[:, 0, t * P:(t + 1) * P], qkvT[:, 1],
                             start=True, stop=True).then_inc(score_done, 1)
                if not first:
                    e.wait_ge(pT_ready, TC * U)
                for s in range(TC):
                    last = e.transpose(bank_t[0][:, s * P:(s + 1) * P], qkvT[:, 2, s * P:(s + 1) * P], mem.ident[:, :])
                last.then_inc(v_turned, 1)
                if u + 1 < UNITS:
                    project_qkv(u + 1)
                e.wait_ge(probs_ready, TC * U + TC)
                for s in range(TC):
                    if s == 1:
                        e.wait_ge(v_ready, U + 1)
                    elif s >= 2:
                        e.wait_ge(pT_ready, TC * U + s - 1)
                    for t in range(TC):
                        last = e.transpose(bank_t[(s + 1) % 2][:, t * P:(t + 1) * P], probs[:, t, s * P:(s + 1) * P],
                                           mem.ident[:, :])
                    last.then_inc(p_turned, 1)
                e.wait_ge(v_ready, U + 1)
                m = 5 * u
                if not first:
                    e.wait_ge(acc_done, TC * U - 1)
                for s in range(TC):
                    e.wait_ge(pT_ready, TC * U + s + 1)
                    last = e.matmul(bank_o[m % 2][:, :], v[:, s], probsT[:, s], start=(s == 0), stop=(s == TC - 1))
                last.then_inc(o_done, 1)
                e.wait_ge(oT_ready, U + 1)
                for t in range(TC):
                    m = 5 * u + 1 + t
                    if t == 0:
                        if not first:
                            e.wait_ge(acc_done, TC * U)
                    elif t >= 2:
                        e.wait_ge(acc_done, TC * U + t - 1)
                    e.matmul(bank_o[m % 2][:, :], oT[:, t * P:(t + 1) * P], out_w[i], start=True, stop=True).then_inc(proj_done, 1)

        @block.tensor
        def _(e):
            pe_pair(e, 0)
            with e.Fori(1, PAIRS) as g:
                pe_pair(e, g)

        def act_pair(e, g):
            for u in range(UNITS):
                i, b = u // B, u % B
                U = UNITS * g + u
                first = isinstance(g, int) and g == 0 and u == 0
                if u == 0:
                    e.wait_ge(bias_ready, g + 1)
                    act_qkv(e, g, 0)
                for t in range(TC):
                    e.wait_ge(max_ready, TC * U + t + 1)
                    if t == 0 and not first:
                        e.wait_ge(p_turned, TC * U)
                    e.activation(probs[:, t], bank_s[t % 2][:, :], ACT.Exp, bias=nmax[:, t:t + 1],
                                 accum_out=rsum[:, t:t + 1]).then_inc(exp_ready, 1)
                if u + 1 < UNITS:
                    act_qkv(e, g, u + 1)
                for s in range(TC):
                    e.wait_ge(p_turned, TC * U + s + 1)
                    if s == 0 and not first:
                        e.wait_ge(o_done, U)
                    e.activation(probsT[:, s], bank_t[(s + 1) % 2][:, :], ACT.Copy).then_inc(pT_ready, 1)
                e.wait_ge(o_done, U + 1)
                if not first:
                    e.wait_ge(proj_done, TC * U)
                e.activation(oT, bank_o[(5 * u) % 2][:, :], ACT.Copy).then_inc(oT_ready, 1)

        def act_qkv(e, g, u):
            i = u // B
            U = UNITS * g + u
            for t in (1, 2):
                e.wait_ge(qkv_done, 3 * U + t + 1)
                e.wait_ge(qkv_ready, 3 * U + t)
                e.activation(qkvT[:, t], bank_qkv[(3 * u + t) % 2][:, :], ACT.Identity,
                             bias=bias_of(i, t)).then_inc(qkv_ready, 1)

        @block.scalar
        def _(e):
            e.preload_act_table(ACT.Exp)
            act_pair(e, 0)
            with e.Fori(1, PAIRS) as g:
                act_pair(e, g)

        def dve_pair(e, g):
            def q_out(u):
                i, U = u // B, UNITS * g + u
                e.wait_ge(qkv_done, 3 * U + 1)
                e.tensor_scalar(qkvT[:, 0], bank_qkv[(3 * u) % 2][:, :], bias_of(i, 0), QSCALE,
                                ALU.add, ALU.mult).then_inc(qkv_ready, 1)

            if not isinstance(g, int):
                e.wait_ge(qkv_ready, 3 * UNITS * g)
            e.tensor_scalar(pair_bias, mem.qkv_bT[:, :, bass.ds(2 * g, 2)], 0.0, None, ALU.add).then_inc(bias_ready, 1)
            e.wait_ge(bias_ready, g + 1)
            for u in range(UNITS):
                i, b = u // B, u % B
                U = UNITS * g + u
                if u == 0:
                    q_out(0)
                for t in range(TC):
                    e.wait_ge(score_done, TC * U + t + 1)
                    e.tensor_reduce(nmax[:, t:t + 1], bank_s[t % 2][:, :], AX.X, ALU.max, negate=True).then_inc(max_ready, 1)
                for t in range(TC):
                    e.wait_ge(exp_ready, TC * U + t + 1)
                    e.reciprocal(rinv[:, t:t + 1], rsum[:, t:t + 1]).then_inc(inv_ready, 1)
                    e.wait_ge(inv_ready, TC * U + t + 1)
                    e.tensor_scalar(probs[:, t], probs[:, t], rinv[:, t:t + 1], None, ALU.mult).then_inc(probs_ready, 1)
                e.wait_ge(v_turned, U + 1)
                if not (isinstance(g, int) and g == 0 and u == 0):
                    e.wait_ge(o_done, U)
                e.tensor_copy(v[:, :, :].rearrange("p s d -> p (s d)"), bank_t[0][:, :]).then_inc(v_ready, 1)
                if u + 1 < UNITS:
                    q_out(u + 1)
                for t in range(TC):
                    e.wait_ge(proj_done, TC * U + t + 1)
                    tile = mem.acc[:, b * TC + t]
                    e.tensor_tensor(tile, tile, bank_o[(5 * u + 1 + t) % 2][:, :], ALU.add).then_inc(acc_done, 1)

        @block.vector
        def _(e):
            e.wait_ge(mem.vec_loaded, 32)
            for n in range(NTILE):
                e.tensor_copy(mem.acc[:, n], mem.out_b[:, :]).then_inc(acc_set, 1)
            e.wait_ge(acc_set, NTILE)
            dve_pair(e, 0)
            with e.Fori(1, PAIRS) as g:
                dve_pair(e, g)



def feed_forward(nc, mem, a):
    w1 = mem.cut(13952, [DC, MLP])
    w2 = mem.cut(0, [MC, D])
    hT = [mem.cut(8192 + i * T, [T]) for i in range(2)]
    norm = mem.work[:, 9216:9216 + 2 * TC * D].rearrange("p (r t d) -> p r t d", r=2, t=TC)
    ffn = [mem.cut(9216 + i * D, [D]) for i in range(TC)]
    with ExitStack() as ctx:
        def sem(name):
            return ctx.enter_context(nc.semaphore(name))

        w2_loaded, gated, resid = sem("w2_loaded"), sem("gated"), sem("resid")
        h_done, hT_ready, y_done, y_out, gated_ffn, x_added = (
            sem(n) for n in ("h_done", "hT_ready", "y_done", "y_out", "gated_ffn", "x_added"))
        ffn_added = sem("ffn_added")
        ln_dve, ln_act, ln_pe, turned, act_out, dve_out = layernorm_engines(nc, ctx, mem, "ln2", mem.acc, 2, norm, lambda e: None)
        bank_h, bank_y = mem.psum[0:2], mem.psum[4:8]
        block = ctx.enter_context(nc.Block())

        @block.sync
        def _(e):
            e.dma_start(w2, a["ffn_w2"].rearrange("(c p) n -> p c n", p=P)).then_inc(w2_loaded, 16)

        @block.gpsimd
        def _(e):
            for t in range(NTILE):
                e.wait_ge(resid, t + 1)
                e.tensor_tensor(mem.tok[:, t], mem.tok[:, t], mem.acc[:, t], ALU.add).then_inc(x_added, 1)

        @block.tensor
        def _(e):
            ln_pe(e)
            e.wait_ge(mem.w1_loaded, 16)
            e.wait_ge(w2_loaded, 16)
            e.wait_ge(act_out, 2 * B)
            e.wait_ge(dve_out, 2 * B)
            def batch(b):
                def hidden(m):
                    if m >= 2:
                        e.wait_ge(hT_ready, MC * b + m - 1)
                    for c in range(DC):
                        last = e.matmul(bank_h[m % 2][:, :], w1[:, c, m * P:(m + 1) * P],
                                        mem.feat[:, c, bass.ds(b, 1)].rearrange("p o t -> p (o t)"),
                                        start=(c == 0), stop=(c == DC - 1))
                    last.then_inc(h_done, 1)

                hidden(0)
                for m in range(MC):
                    if m + 1 < MC:
                        hidden(m + 1)
                    e.wait_ge(hT_ready, MC * b + m + 1)
                    for t in range(TC):
                        if m == 0 and t == 0 and not isinstance(b, int):
                            e.wait_ge(y_out, TC * b)
                        last = e.matmul(bank_y[t][:, :], hT[m % 2][:, t * P:(t + 1) * P], w2[:, m],
                                        start=(m == 0), stop=(m == MC - 1))
                    last.then_inc(y_done, 1)

            batch(0)
            with e.Fori(1, B) as b:
                batch(b)

        @block.scalar
        def _(e):
            ln_act(e)
            e.preload_act_table(ACT.Gelu)
            with e.Fori(0, B) as b:
                for m in range(MC):
                    e.wait_ge(h_done, MC * b + m + 1)
                    if m >= 2:
                        e.wait_ge(y_done, MC * b + m - 1)
                    e.activation(hT[m % 2], bank_h[m % 2][:, :], ACT.Gelu, bias=mem.b1T[:, m:m + 1]).then_inc(hT_ready, 1)

        @block.vector
        def _(e):
            def gate_residual(e, b):
                for t in range(b * TC, (b + 1) * TC):
                    e.tensor_tensor(mem.acc[:, t], mem.acc[:, t], mem.gate[:, 0, b], ALU.mult).then_inc(gated, 1)
                for t in range(b * TC, (b + 1) * TC):
                    e.wait_ge(gated, t + 1)
                    e.tensor_tensor(mem.acc[:, t], mem.acc[:, t], mem.tok[:, t], ALU.add).then_inc(resid, 1)
                e.wait_ge(resid, (b + 1) * TC)

            ln_dve(e, gate_residual)
            e.wait_ge(turned, DC * B)
            e.wait_ge(x_added, NTILE)
            def batch(b):
                e.wait_ge(y_done, MC * b + MC)
                if not isinstance(b, int):
                    e.wait_ge(ffn_added, TC * b)
                for t in range(TC):
                    e.tensor_tensor(ffn[t], bank_y[t][:, :], mem.b2[:, :], ALU.add).then_inc(y_out, 1)
                gate = mem.gate[:, 1, bass.ds(b, 1)].rearrange("p o d -> p (o d)")
                for t in range(TC):
                    e.wait_ge(y_out, TC * b + t + 1)
                    e.tensor_tensor(ffn[t], ffn[t], gate, ALU.mult).then_inc(gated_ffn, 1)
                for t in range(TC):
                    e.wait_ge(gated_ffn, TC * b + t + 1)
                    tile = mem.tok[:, bass.ds(TC * b + t, 1)].rearrange("p o d -> p (o d)")
                    e.tensor_tensor(tile, tile, ffn[t], ALU.add).then_inc(ffn_added, 1)

            batch(0)
            with e.Fori(1, B) as b:
                batch(b)


def convolution(nc, mem, a):
    coupling = mem.cut(0, [DC, D])
    couplingT = mem.cut(2048, [DC, D])
    with ExitStack() as ctx:
        def sem(name):
            return ctx.enter_context(nc.semaphore(name))

        turned, copied, tap, tap1 = sem("x_turned"), sem("x_copied"), sem("tap"), sem("tap_first")
        c_turned = sem("coupling_turned")
        bank = mem.psum[0:4]
        block = ctx.enter_context(nc.Block())

        @block.sync
        def _(e):
            e.dma_start(coupling, a["coupling"].rearrange("(c p) n -> p c n", p=P)).then_inc(mem.coupling_loaded, 16)

        @block.tensor
        def _(e):
            n = 0
            for b in range(B):
                for c in range(DC):
                    if n >= 4:
                        e.wait_ge(tap, n - 3)
                    for t in range(TC):
                        last = e.transpose(bank[n % 4][:, t * P:(t + 1) * P], mem.tok[:, b * TC + t, c * P:(c + 1) * P],
                                           mem.ident[:, :])
                    last.then_inc(turned, 1)
                    n += 1
            e.wait_ge(mem.coupling_loaded, 16)
            for c in range(DC):
                for r in range(DC):
                    last = e.transpose(mem.psum[4 + c][:, r * P:(r + 1) * P], coupling[:, r, c * P:(c + 1) * P],
                                       mem.ident[:, :])
                last.then_inc(c_turned, 1)

        @block.scalar
        def _(e):
            for n in range(B * DC):
                b, c = n // DC, n % DC
                e.wait_ge(turned, n + 1)
                e.activation(mem.feat[:, c, b], bank[n % 4][:, :], ACT.Identity,
                             bias=mem.convbT[:, c:c + 1]).then_inc(copied, 1)
            for c in range(DC):
                e.wait_ge(c_turned, c + 1)
                e.activation(couplingT[:, c], mem.psum[4 + c][:, :], ACT.Copy).then_inc(copied, 1)

        @block.vector
        def _(e):
            for n in range(B * DC):
                b, c = n // DC, n % DC
                x = bank[n % 4]
                e.wait_ge(copied, n + 1)
                for back in range(B):
                    if back:
                        e.wait_ge(tap1, n * (B - 1) + back)
                    out = mem.feat[:, c, b, back:]
                    e.scalar_tensor_tensor(out=out, in0=x[:, 0:T - back], scalar=mem.condT[:, c, B - 1 - back:B - back],
                                           in1=out, op0=ALU.mult, op1=ALU.add).then_inc(tap if back == B - 1 else tap1, 1)



def coupled_scan(nc, mem, a):
    N = DC * B
    QT = P // 4
    couplingT = mem.cut(2048, [DC, D])
    at = [4096]

    def state(n=N):
        at[0] += n
        return mem.cut(at[0] - n, [n])

    q, q2, q3, q4, q_new = (state() for _ in range(5))
    p, p2, p3, p4, p_new = (state() for _ in range(5))
    v = [state() for _ in range(4)]
    dq = [state() for _ in range(3)]
    square, cubic, drive, bias, dq_sum, v_mid, v_ends, v_sum, lessp0, lessp, lead_dq = (
        state() for _ in range(11))
    lead, base, partial = ([state() for _ in range(2)] for _ in range(3))
    tanh_q = state()
    back = [state(P) for _ in range(2)]
    idle = mem.cut(at[0], [P]).bitcast(BF16)[:, 0:P]
    x = mem.feat[:, :, :, :].rearrange("p c b t -> p (c b) t")
    C = [H_STEP / 2, H_STEP / 2, H_STEP, H_STEP / 6]
    Q, PP = [q, q2, q3, q4], [p, p2, p3, p4]
    with ExitStack() as ctx:
        def sem(name):
            return ctx.enter_context(nc.semaphore(name))

        set_up, vec, q_ready, q_clipped, v_ready, p_ready, square_ready, lessp_ready = (
            sem(n) for n in ("scan_set_up", "vec", "q_ready", "q_clipped", "v_ready", "p_ready", "square_ready",
                             "lessp_ready"))
        tanh_ready, m_ready, dq_ready, v_mid_ready, v_ends_ready = (
            sem(n) for n in ("tanh_ready", "m_ready", "dq_ready", "v_mid_ready", "v_ends_ready"))
        STEPS = 6
        assert (T - 2) % STEPS == 0
        block = ctx.enter_context(nc.Block())

        @block.scalar
        def _(e):
            e.preload_act_table(ACT.Tanh)
            with e.Fori(0, T) as t:
                for i in range(4):
                    e.wait_ge(q_ready, 4 * t + i + 1)
                    e.activation(tanh_q, Q[i] if i else q_new, ACT.Tanh).then_inc(tanh_ready, 1)

        @block.tensor
        def _(e):
            e.wait_ge(set_up, 4 + B)
            with e.Fori(0, T) as t:
                for i in range(4):
                    e.wait_ge(tanh_ready, 4 * t + i + 1)
                    for c in range(DC):
                        for j in range(4):
                            cols = couplingT[:, c].rearrange("p (s j k) -> p j s k", s=DC, j=4)[:, j]
                            last = e.matmul(mem.psum[i % 2][QT * j:QT * j + B, 0:P], tanh_q[:, B * c:B * c + B], cols,
                                            start=(c == 0), stop=(c == DC - 1), tile_position=(0, QT * j))
                    last.then_inc(m_ready, 1)
                    for _ in range(KEEP_WARM):
                        e.matmul(mem.psum[2][:, 0:P], idle, idle, start=True, stop=True)

        @block.gpsimd
        def _(e):
            e.wait_ge(set_up, 5 + B)
            with e.Fori(0, T) as t:
                for i in range(4):
                    if i == 0:
                        e.wait_ge(q_clipped, t + 1)
                    else:
                        e.wait_ge(q_ready, 4 * t + i + 1)
                    e.tensor_tensor(square, Q[i], Q[i], ALU.mult).then_inc(square_ready, 1)
                    if i < 3:
                        e.wait_ge(p_ready, 3 * t + i + 1)
                        e.tensor_tensor(lessp, drive, PP[i + 1], ALU.subtract).then_inc(lessp_ready, 1)
                    if i > 0:
                        e.tensor_tensor(dq[i - 1], Q[i], q, ALU.subtract).then_inc(dq_ready, 1)
                    if i == 2:
                        e.wait_ge(v_ready, 4 * t + 3)
                        e.tensor_tensor(v_mid, v[1], v[2], ALU.add).then_inc(v_mid_ready, 1)
                    if i == 3:
                        e.wait_ge(v_ready, 4 * t + 4)
                        e.tensor_tensor(v_ends, v[0], v[3], ALU.add).then_inc(v_ends_ready, 1)

        @block.vector
        def _(e):
            e.memset(mem.psum[0][:, 0:P], 0.0).then_inc(set_up, 1)
            e.memset(mem.psum[1][:, 0:P], 0.0).then_inc(set_up, 1)
            e.memset(idle, 0.0).then_inc(set_up, 1)
            cond = mem.condT[:, :, :].rearrange("p c b -> p (c b)")
            e.tensor_scalar(p, cond, -P_SHIFT, None, ALU.add).then_inc(set_up, 1)
            for b in range(B):
                e.tensor_scalar(bias.rearrange("p (c b) -> p c b", b=B)[:, :, b], mem.cbiasT, -P_SHIFT, None,
                                ALU.add).then_inc(set_up, 1)
            e.wait_ge(set_up, 4 + B)
            e.tensor_copy(q_new, cond).then_inc(q_ready, 1)
            e.tensor_tensor(drive, x[:, :, 0], bias, ALU.add).then_inc(set_up, 1)
            e.tensor_copy(q, cond).then_inc(q_clipped, 1)
            e.wait_ge(set_up, 5 + B)
            e.wait_ge(q_clipped, 1)
            OPS = 29

            def fma(out, in0, scalar, in1, op1=ALU.add):
                return e.scalar_tensor_tensor(out=out, in0=in0, scalar=scalar, in1=in1, op0=ALU.mult, op1=op1)

            def x_at(t):
                return x[:, :, bass.ds(t, 1)].rearrange("p n o -> p (n o)")

            def step(t, first=False, last=False):
                before = 0 if first else OPS * t - 1
                done = {}
                count = [0]

                def signal(name, instruction):
                    count[0] += 1
                    done[name] = count[0]
                    instruction.then_inc(vec, 1)

                def need(*names):
                    e.wait_ge(vec, before + max(done[n] for n in names))

                for i in range(4):
                    qi, pi, c, even = Q[i], PP[i], C[i], i % 2
                    fma(v[i], pi, -BETA, qi).then_inc(v_ready, 1)
                    if i == 0:
                        signal("lessp0", e.tensor_tensor(lessp0, drive, p, ALU.subtract))
                    if i < 3:
                        e.wait_ge(v_ready, 4 * t + i + 1)
                        fma(PP[i + 1], v[i], c * EPSILON, p).then_inc(p_ready, 1)
                    if i == 0:
                        need("lessp0")
                        signal("lead0", fma(lead[0], lessp0, c, q))
                    e.wait_ge(square_ready, 4 * t + i + 1)
                    signal("cubic", fma(cubic, square, -1 / 3, qi, ALU.mult))
                    if i < 3:
                        need(f"lead{i}")
                        signal("partial", fma(partial[even], qi, c, lead[even]))
                    if i == 1 and not first:
                        signal("trace", e.tensor_tensor(x_at(t - 1), x_at(t - 1), q, ALU.add))
                    if i < 3:
                        need("partial", "cubic")
                        signal("base", fma(base[even], cubic, c, partial[even]))
                        e.wait_ge(lessp_ready, 3 * t + i + 1)
                        signal(f"lead{i + 1}", fma(lead[1 - even], lessp, C[i + 1], q))
                    if i == 2:
                        e.wait_ge(dq_ready, 3 * t + 2)
                        signal("dq_sum", fma(dq_sum, dq[1], 2.0, dq[0]))
                        need("dq_sum", "lead3")
                        signal("lead_dq", fma(lead_dq, dq_sum, 1 / 3, lead[1]))
                    if i == 3:
                        need("lead_dq")
                        signal("partial3", fma(partial[0], qi, c, lead_dq))
                        if not last:
                            signal("drive", e.tensor_tensor(drive, x_at(t + 1), bias, ALU.add))
                        need("partial3", "cubic")
                        signal("partial", fma(partial[1], cubic, c, partial[0]))
                        e.wait_ge(v_mid_ready, t + 1)
                        e.wait_ge(v_ends_ready, t + 1)
                        signal("v_sum", fma(v_sum, v_mid, 2.0, v_ends))
                        need("partial")
                        e.wait_ge(dq_ready, 3 * t + 3)
                        signal("base", fma(base[1], dq[2], 1 / 3, partial[1]))
                        need("v_sum")
                        signal("p_new", fma(p_new, v_sum, C[3] * EPSILON, p))
                        need("p_new")
                        signal("p", e.tensor_scalar(p, p_new, CLAMP - P_SHIFT, -CLAMP - P_SHIFT, ALU.min, ALU.max))
                    e.wait_ge(m_ready, 4 * t + i + 1)
                    signal("back", e.transpose(back[even], mem.psum[even][:, 0:P]))
                    need("back", "base")
                    coupled = back[even].rearrange("p (c r) -> p c r", c=DC)[:, :, 0:B]
                    to = Q[i + 1] if i < 3 else q_new
                    fma(to.rearrange("p (c b) -> p c b", c=DC), coupled, c,
                        base[even].rearrange("p (c b) -> p c b", c=DC)).then_inc(q_ready, 1)
                    e.wait_ge(q_ready, 4 * t + i + 2)
                e.tensor_scalar(q, q_new, CLAMP, -CLAMP, ALU.min, ALU.max).then_inc(q_clipped, 1)
                e.wait_ge(q_clipped, t + 2)
                assert last or count[0] == OPS - first, count

            step(0, first=True)
            with e.Fori(0, (T - 2) // STEPS) as k:
                for n in range(STEPS):
                    step(k * STEPS + (1 + n))
            step(T - 1, last=True)
            e.tensor_tensor(x_at(T - 1), x_at(T - 1), q, ALU.add).then_inc(vec, 1)


def top_k(nc, mem, a):
    at = [0]

    def place(*shape):
        n = 1
        for k in shape:
            n *= k
        at[0] += n
        return mem.cut(at[0] - n, list(shape))

    ones, before = place(P), place(P)
    eq, rank, one_row = place(NTILE, D), place(2, D), place(D)
    nmax, rsum, rinv = place(NTILE), place(NTILE), place(NTILE)
    count, total, bit_value, above, left = (place(B) for _ in range(5))
    candidate, found, bit, taken = (place(B).bitcast(I32) for _ in range(4))
    row_count, row_before, offset = place(NTILE), place(NTILE), place(NTILE)
    emb_t = mem.gate[:, 0]
    with ExitStack() as ctx:
        def sem(name):
            return ctx.enter_context(nc.semaphore(name))

        emb_loaded, const, turned, copied, max_ready, exp_ready, inv_ready, soft, prod, adj_ready = (
            sem(n) for n in ("emb_loaded", "topk_const", "x4_turned", "x4_copied", "row_max", "row_exp", "row_inv",
                             "row_soft", "adj_product", "adj_ready"))
        counted, summed, chosen = sem("counted"), sem("summed"), sem("chosen")
        tie, tie_sum, ranked, picked, masked, stored = (
            sem(n) for n in ("tie", "tie_sum", "ranked", "picked", "masked", "stored"))
        bank = mem.psum[0:4]
        block = ctx.enter_context(nc.Block())
        BITS = 31

        @block.sync
        def _(e):
            for b in range(B):
                e.dma_start(emb_t[:, b], a["cond"][b:b + 1].broadcast_to((P, D))).then_inc(emb_loaded, 16)
            y = a["out"].rearrange("b (t p) d -> b p t d", p=P)
            for b in range(B):
                e.wait_ge(masked, TC * (b + 1))
                e.dma_start(y[b], mem.tok[:, b * TC:(b + 1) * TC]).then_inc(stored, 16)
            e.wait_ge(stored, 16 * B)

        @block.gpsimd
        def _(e):
            e.memset(ones, 1.0).then_inc(const, 1)
            e.memset(before, 1.0).then_inc(const, 1)
            e.wait_ge(const, 2)
            e.affine_select(out=before, in_=before, compare_op=ALU.is_gt, fill=0.0, base=0,
                            pattern=[[1, P]], channel_multiplier=-1).then_inc(const, 1)
            for n in range(NTILE):
                t = n % TC
                e.wait_ge(prod, n + 1)
                diag = mem.acc[:, n, t * P:(t + 1) * P]
                e.affine_select(out=diag, in_=diag, compare_op=ALU.not_equal, fill=-3.0e38, base=0,
                                pattern=[[-1, P]], channel_multiplier=1).then_inc(adj_ready, 1)
            for n in range(NTILE):
                e.wait_ge(picked, n + 1)
                e.tensor_tensor(mem.tok[:, n], mem.tok[:, n], eq[:, n], ALU.add).then_inc(masked, 1)

        @block.tensor
        def _(e):
            for n in range(NTILE):
                b, t = n // TC, n % TC
                if n >= 4:
                    e.wait_ge(copied, n - 3)
                for c in range(DC):
                    last = e.transpose(bank[n % 4][:, c * P:(c + 1) * P], mem.feat[:, c, b, t * P:(t + 1) * P],
                                       mem.ident[:, :])
                last.then_inc(turned, 1)
            e.wait_ge(const, 3)
            e.wait_ge(counted, 1)
            e.matmul(mem.psum[4][:, 0:B], ones, count, start=True, stop=True).then_inc(summed, 1)
            with e.Fori(0, BITS) as k:
                e.wait_ge(counted, k + 2)
                e.matmul(mem.psum[4][:, 0:B], ones, count, start=True, stop=True).then_inc(summed, 1)
            e.wait_ge(counted, BITS + 2)
            e.matmul(mem.psum[4][:, 0:B], ones, count, start=True, stop=True).then_inc(summed, 1)
            e.wait_ge(tie, TC - 1)
            e.matmul(mem.psum[5][:, 0:NTILE], before, row_count, start=True, stop=False)
            e.matmul(mem.psum[5][:, 0:NTILE], ones, row_before, start=False, stop=True).then_inc(tie_sum, 1)

        @block.scalar
        def _(e):
            e.preload_act_table(ACT.Exp)
            for n in range(NTILE + 1):
                if n < NTILE:
                    e.wait_ge(turned, n + 1)
                    e.activation(mem.tok[:, n], bank[n % 4][:, :], ACT.Copy).then_inc(copied, 1)
                if n >= 1:
                    e.wait_ge(max_ready, n)
                    e.activation(mem.acc[:, n - 1], mem.tok[:, n - 1], ACT.Exp, bias=nmax[:, n - 1:n],
                                 accum_out=rsum[:, n - 1:n]).then_inc(exp_ready, 1)

        @block.vector
        def _(e):
            e.wait_ge(emb_loaded, 16 * B)

            def weigh(n):
                b = n // TC
                e.wait_ge(exp_ready, n + 1)
                e.reciprocal(rinv[:, n:n + 1], rsum[:, n:n + 1]).then_inc(inv_ready, 1)
                e.wait_ge(inv_ready, n + 1)
                e.tensor_scalar(mem.acc[:, n], mem.acc[:, n], rinv[:, n:n + 1], T ** -0.5, ALU.mult, ALU.mult).then_inc(soft, 1)
                e.wait_ge(soft, n + 1)
                e.scalar_tensor_tensor(out=mem.acc[:, n], in0=emb_t[:, b], scalar=mem.emb_s[:, n:n + 1],
                                       in1=mem.acc[:, n], op0=ALU.mult, op1=ALU.mult).then_inc(prod, 1)

            for n in range(NTILE):
                e.wait_ge(copied, n + 1)
                e.tensor_reduce(nmax[:, n:n + 1], mem.tok[:, n], AX.X, ALU.max, negate=True).then_inc(max_ready, 1)
                if n >= 1:
                    weigh(n - 1)
            weigh(NTILE - 1)
            steps = [0]

            def chain(instruction):
                instruction.then_inc(chosen, 1)
                steps[0] += 1
                e.wait_ge(chosen, steps[0])

            def count_in(b, threshold, compare):
                flat = eq[:, b * TC:(b + 1) * TC].rearrange("p t d -> p (t d)")
                return e.tensor_scalar(flat, mem.acc[:, b * TC:(b + 1) * TC].rearrange("p t d -> p (t d)"), threshold,
                                       None, compare, ALU.add, accum_out=count[:, b:b + 1])

            e.wait_ge(adj_ready, NTILE)
            for b in range(B):
                last = count_in(b, 0.0, ALU.is_ge)
            last.then_inc(counted, 1)
            chain(e.memset(one_row, 1.0))
            chain(e.memset(bit, 1 << 30))
            chain(e.memset(bit_value, float(1 << 30)))
            e.wait_ge(summed, 1)
            chain(e.tensor_scalar(found, mem.psum[4][:, 0:B], float(TOPK), -1.0, ALU.is_lt, ALU.mult))
            head = steps[0]
            CHAIN = 5
            with e.Fori(0, BITS) as k:
                def link(n, instruction):
                    instruction.then_inc(chosen, 1)
                    e.wait_ge(chosen, CHAIN * k + head + n)

                link(1, e.tensor_tensor(candidate, found, bit, ALU.bitwise_xor))
                for b in range(B):
                    last = count_in(b, candidate[:, b:b + 1].bitcast(F32), ALU.is_ge)
                last.then_inc(counted, 1)
                link(2, e.tensor_scalar(bit, bit, 1, None, ALU.logical_shift_right))
                e.wait_ge(summed, k + 2)
                link(3, e.scalar_tensor_tensor(out=taken, in0=mem.psum[4][:, 0:B], scalar=float(TOPK), in1=bit_value,
                                               op0=ALU.is_ge, op1=ALU.mult))
                link(4, e.tensor_tensor(found, found, taken, ALU.bitwise_xor))
                link(5, e.tensor_scalar(bit_value, bit_value, 0.5, None, ALU.mult))
            steps[0] = head + CHAIN * BITS
            threshold = found.bitcast(F32)
            for b in range(B):
                last = count_in(b, threshold[:, b:b + 1], ALU.is_gt)
            last.then_inc(counted, 1)
            e.wait_ge(counted, BITS + 2)
            for n in range(NTILE):
                b = n // TC
                last = e.tensor_scalar(eq[:, n], mem.acc[:, n], threshold[:, b:b + 1], None, ALU.is_equal, ALU.add,
                                       accum_out=row_count[:, n:n + 1])
            chain(last)
            rows, sums = (r.rearrange("p (b t) -> p t b", b=B) for r in (row_count, row_before))
            chain(e.memset(sums[:, 0], 0.0))
            for t in range(1, TC):
                e.tensor_tensor(sums[:, t], sums[:, t - 1], rows[:, t - 1], ALU.add).then_inc(tie, 1)
                e.wait_ge(tie, t)
            e.wait_ge(summed, BITS + 2)
            chain(e.tensor_scalar(left, mem.psum[4][:, 0:B], -1.0, float(TOPK), ALU.mult, ALU.add))
            e.wait_ge(tie_sum, 1)
            chain(e.tensor_copy(offset, mem.psum[5][:, 0:NTILE]))
            for n in range(NTILE):
                b = n // TC
                e.tensor_tensor_scan(rank[:, n % 2], one_row, eq[:, n], offset[:, n:n + 1], ALU.mult, ALU.add).then_inc(ranked, 1)
                e.wait_ge(ranked, 2 * n + 1)
                e.scalar_tensor_tensor(out=eq[:, n], in0=rank[:, n % 2], scalar=left[:, b:b + 1], in1=eq[:, n],
                                       op0=ALU.is_le, op1=ALU.mult).then_inc(ranked, 1)
                e.wait_ge(ranked, 2 * n + 2)
                e.scalar_tensor_tensor(out=eq[:, n], in0=mem.acc[:, n], scalar=threshold[:, b:b + 1], in1=eq[:, n],
                                       op0=ALU.is_gt, op1=ALU.add).then_inc(picked, 1)


INPUTS = {"x": "x", "cond": "cond_2048", "fside": "fside_BxSx1_0", "ada_w": "L0_cond_ada_w", "ada_b": "L0_cond_ada_b",
          "qkv_w": "L0_cond_qkv_w", "qkv_b": "L0_cond_qkv_b", "out_w": "L0_cond_out_w", "out_b": "L0_cond_out_b",
          "ffn_w1": "L0_cond_ffn_w1", "ffn_b1": "L0_cond_ffn_b1", "ffn_w2": "L0_cond_ffn_w2", "ffn_b2": "L0_cond_ffn_b2",
          "conv_b": "L1_cond_b", "coupling": "L2_cond_coupling", "bias": "L2_cond_bias"}


def program(nc, a):
    with ExitStack() as ctx:
        mem = Memory(nc, ctx)
        prepare(nc, mem, a)
        attention(nc, mem, a)
        feed_forward(nc, mem, a)
        convolution(nc, mem, a)
        coupled_scan(nc, mem, a)
        top_k(nc, mem, a)


def kernel(**inputs):
    import numpy as np
    import concourse.bacc as bacc
    from concourse.bass_utils import run_bass_kernel_spmd

    nc = bacc.Bacc("TRN2", target_bir_lowering=False, num_devices=1)
    arrays, a = {}, {}
    for short, name in INPUTS.items():
        v = np.ascontiguousarray(inputs[name])
        arrays["in_" + name] = v
        a[short] = nc.dram_tensor("in_" + name, v.shape, mybir.dt.from_np(v.dtype), kind="ExternalInput").ap()
    a["out"] = nc.dram_tensor("out", (B, T, D), F32, kind="ExternalOutput").ap()
    program(nc, a)
    r = run_bass_kernel_spmd(nc, [arrays], core_ids=[0])
    return r.results[0]["out"]
```

```python
import concourse.bass as bass
from concourse import mybir
from contextlib import ExitStack

F32 = mybir.dt.float32
I32 = mybir.dt.int32
BF16 = mybir.dt.bfloat16
F32R = mybir.dt.float32r
ACT = mybir.ActivationFunctionType
ALU = mybir.AluOpType
AX = mybir.AxisListType

P = 128
B, T, D = 4, 512, 512
TC, DC = T // P, D // P
NTILE = B * TC
HEADS, DH = 16, 128
INNER = HEADS * DH
MLP = 2048
MC = MLP // P
QSCALE = DH ** -0.5
LN_EPS = 1e-6
TOPK = 5120
H_STEP, EPSILON, ALPHA, BETA, CLAMP = 0.01, 0.08, 0.7, 0.8, 20.0
P_SHIFT = ALPHA / BETA
KEEP_WARM = 8


VECS = MC + NTILE + 2 * DC + 3 * HEADS


class Memory:

    def __init__(self, nc, ctx):
        self.nc, self.ends = nc, {}

        def sb(name, shape, dt=F32):
            tensor = ctx.enter_context(nc.sbuf_tensor(name, shape, dt))
            self.ends[name] = nc.sbuf_base
            return tensor

        self.tok = sb("tok", [P, NTILE, D])
        self.acc = sb("acc", [P, NTILE, D])
        self.feat = sb("feat", [P, DC, B, T])
        self.gate = sb("gate", [P, 2, B, D])
        self.work = sb("work", [P, 22400])
        self.ident = sb("ident", [P, P])
        self.sel = sb("sel", [B, B, P])
        self.condT = sb("condT", [P, DC, B])
        self.adaT = sb("adaT", [P, 4, DC, B])
        self.out_b = sb("out_b", [P, D])
        self.b2 = sb("b2", [P, D])
        self.vecT = sb("vecT", [P, VECS])
        self.b1T = self.vecT[:, 0:MC]
        self.emb_s = self.vecT[:, MC:MC + NTILE]
        self.convbT = self.vecT[:, 32:32 + DC]
        self.cbiasT = self.vecT[:, 36:36 + DC]
        self.qkv_bT = self.vecT[:, 40:40 + 3 * HEADS].rearrange("p (t h) -> p t h", t=3)
        self.stats = sb("stats", [P, NTILE, 6])
        self.mv = sb("mv", [P, NTILE, 2])
        self.rstd = sb("rstd", [P, 2, NTILE])
        self.small = sb("small", [P, 64])
        self.psum = [ctx.enter_context(nc.psum_tensor(f"bank{i}", [P, 512], F32)) for i in range(8)]
        self.const_ready = ctx.enter_context(nc.semaphore("const_ready"))
        self.vec_loaded = ctx.enter_context(nc.semaphore("vec_loaded"))
        self.vecT_ready = ctx.enter_context(nc.semaphore("vecT_ready"))
        self.x_reloaded = [ctx.enter_context(nc.semaphore(f"x_reloaded{b}")) for b in range(B)]
        self.w1_loaded = ctx.enter_context(nc.semaphore("w1_loaded"))
        self.coupling_loaded = ctx.enter_context(nc.semaphore("coupling_loaded"))

    def rounded(self, name, within, start, shape):
        n = 1
        for k in within.shape[1:]:
            n *= k
        first = self.ends[within.name] - 4 * (n - start)
        return self.nc.alloc_sbuf_tensor_at(name, [P] + shape, F32R, offset=first)

    def cut(self, start, shape):
        n = 1
        for s in shape:
            n *= s
        flat = self.work[:, start:start + n]
        if len(shape) == 1:
            return flat
        names = "abc"[:len(shape)]
        return flat.rearrange(f"p ({' '.join(names)}) -> p {' '.join(names)}",
                              **{k: v for k, v in zip(names, shape)})


def layernorm_engines(nc, ctx, mem, block_name, src, shift, norm, cond_ready):
    def sem(name):
        return ctx.enter_context(nc.semaphore(f"{block_name}_{name}"))

    stat, var_ready, std_ready, norm_ready, turned, act_out, dve_out = (
        sem(n) for n in ("stat", "var_ready", "std_ready", "norm_ready", "turned", "act_out", "dve_out"))
    bank = mem.psum[4:8]

    def dve(e, src_ready):
        for b in range(B):
            src_ready(e, b)
            tiles = range(b * TC, (b + 1) * TC)
            for t in tiles:
                e.bn_stats(mem.stats[:, t], src[:, t]).then_inc(stat, 1)
            for n, t in enumerate(tiles):
                e.wait_ge(stat, (2 * b) * TC + n + 1)
                e.bn_aggr(mem.mv[:, t], mem.stats[:, t]).then_inc(stat, 1)
            e.wait_ge(stat, (2 * b + 2) * TC)
            e.tensor_scalar(mem.rstd[:, 0, b * TC:(b + 1) * TC], mem.mv[:, b * TC:(b + 1) * TC, 1],
                            LN_EPS, None, ALU.add).then_inc(var_ready, 1)
            e.wait_ge(std_ready, 2 * b + 1)
            e.reciprocal(mem.rstd[:, 1, b * TC:(b + 1) * TC],
                         mem.rstd[:, 0, b * TC:(b + 1) * TC]).then_inc(std_ready, 1)
            e.wait_ge(std_ready, 2 * b + 2)
            if b >= 2:
                e.wait_ge(turned, DC * (b - 1))
            for n, t in enumerate(tiles):
                e.tensor_scalar(norm[:, b % 2, n], src[:, t], mem.mv[:, t, 0:1],
                                mem.rstd[:, 1, t:t + 1], ALU.subtract, ALU.mult).then_inc(norm_ready, 1)
            cond_ready(e)
            for c in (1, 3):
                e.wait_ge(turned, DC * b + c + 1)
                e.tensor_scalar(mem.feat[:, c, b], bank[c][:, :], mem.adaT[:, shift + 1, c, b:b + 1],
                                mem.adaT[:, shift, c, b:b + 1], ALU.mult, ALU.add).then_inc(dve_out, 1)

    def act(e):
        for b in range(B):
            e.wait_ge(var_ready, b + 1)
            e.activation(mem.rstd[:, 0, b * TC:(b + 1) * TC], mem.rstd[:, 0, b * TC:(b + 1) * TC],
                         ACT.Sqrt).then_inc(std_ready, 1)
            cond_ready(e)
            for c in (0, 2):
                e.wait_ge(turned, DC * b + c + 1)
                e.activation(mem.feat[:, c, b], bank[c][:, :], ACT.Identity,
                             bias=mem.adaT[:, shift, c, b:b + 1],
                             scale=mem.adaT[:, shift + 1, c, b:b + 1]).then_inc(act_out, 1)

    def pe(e):
        for b in range(B):
            e.wait_ge(norm_ready, TC * (b + 1))
            for c in range(DC):
                if b >= 1:
                    e.wait_ge(act_out if c % 2 == 0 else dve_out, 2 * (b - 1) + c // 2 + 1)
                for n in range(TC):
                    last = e.transpose(bank[c][:, n * P:(n + 1) * P], norm[:, b % 2, n, c * P:(c + 1) * P],
                                       mem.ident[:, :])
                last.then_inc(turned, 1)

    return dve, act, pe, turned, act_out, dve_out


def prepare(nc, mem, a):
    ada_w = mem.cut(0, [DC, 6 * D])
    ada = mem.cut(12288, [6 * D])[0:B]
    norm = mem.work[:, 15360:15360 + 2 * TC * D].rearrange("p (r t d) -> p r t d", r=2, t=TC)
    rows = mem.gate[0:B].rearrange("p k b d -> p (k b d)")
    ada_b, cond = rows[:, 0:6 * D], rows[:, 6 * D:7 * D]
    vec_rows = mem.cut(19456, [P])[0:VECS]
    with ExitStack() as ctx:
        def sem(name):
            return ctx.enter_context(nc.semaphore(name))

        x_loaded = [sem(f"x_loaded{b}") for b in range(B)]
        w_loaded = [sem(f"ada_w_loaded{n}") for n in range(6)]
        cond_loaded, adab_loaded, zeroed = sem("cond_loaded"), sem("adab_loaded"), sem("zeroed")
        rows_loaded, rows_turned = sem("rows_loaded"), sem("rows_turned")
        cond_turned, condT_ready = sem("cond_turned"), sem("condT_ready")
        ada_done, ada_ready, ada_turned, adaT_ready = (sem(n) for n in ("ada_done", "ada_ready", "ada_turned", "adaT_ready"))
        gate_done, gate_ready = sem("gate_done"), sem("gate_ready")
        turned_bank, bank = mem.psum[2], mem.psum
        PARTS = (0, 1, 3, 4)

        def cond_ready(e):
            e.wait_ge(adaT_ready, 4)

        ln_dve, ln_act, ln_pe, *_ = layernorm_engines(nc, ctx, mem, "ln1", mem.tok, 0, norm, cond_ready)
        block = ctx.enter_context(nc.Block())

        @block.sync
        def _(e):
            e.dma_start(cond, a["cond"]).then_inc(cond_loaded, 16)
            e.dma_start(ada_b, a["ada_b"].rearrange("(o n) -> o n", o=1).broadcast_to((B, 6 * D))).then_inc(adab_loaded, 16)
            at = 0
            for name in ("ffn_b1", "fside", "conv_b", "bias", "qkv_b"):
                v = a[name].rearrange("b t o -> (b t o)") if name == "fside" else a[name]
                n = v.shape[0] // P
                e.dma_start(vec_rows[at:at + n], v.rearrange("(c p) -> c p", p=P)).then_inc(rows_loaded, 16)
                at += n
            w = a["ada_w"].rearrange("(c p) n -> p c n", p=P)
            x = a["x"].rearrange("b (t p) d -> b p t d", p=P)
            for n in range(6):
                if n < B:
                    e.dma_start(mem.tok[:, n * TC:(n + 1) * TC], x[n]).then_inc(x_loaded[n], 16)
                e.dma_start(ada_w[:, :, n * D:(n + 1) * D], w[:, :, n * D:(n + 1) * D]).then_inc(w_loaded[n], 16)

        @block.gpsimd
        def _(e):
            e.memset(mem.ident[:, :], 0.0).then_inc(zeroed, 1)
            e.memset(mem.sel[:, :, :], 0.0).then_inc(zeroed, 1)
            e.wait_ge(zeroed, 2)
            e.affine_select(out=mem.ident[:, :], in_=mem.ident[:, :], compare_op=ALU.not_equal, fill=1.0,
                            base=0, pattern=[[-1, P]], channel_multiplier=1).then_inc(mem.const_ready, 1)
            e.affine_select(out=mem.sel[:, :, :], in_=mem.sel[:, :, :], compare_op=ALU.not_equal, fill=1.0,
                            base=0, pattern=[[-1, B], [0, P]], channel_multiplier=1).then_inc(mem.const_ready, 1)

        @block.scalar
        def _(e):
            row = "(o n) -> o n"
            e.dma_start(mem.out_b[:, :], a["out_b"].rearrange(row, o=1).broadcast_to((P, D))).then_inc(mem.vec_loaded, 16)
            e.dma_start(mem.b2[:, :], a["ffn_b2"].rearrange(row, o=1).broadcast_to((P, D))).then_inc(mem.vec_loaded, 16)
            ln_act(e)
            for k in range(2):
                for b in range(B):
                    e.wait_ge(gate_done, k * B + b + 1)
                    e.activation(mem.gate[:, k, b], bank[b % 2][:, :], ACT.Copy).then_inc(gate_ready, 1)

        @block.tensor
        def _(e):
            e.wait_ge(mem.const_ready, 2)
            e.wait_ge(cond_loaded, 16)
            for c in range(DC):
                last = e.transpose(turned_bank[:, c * B:(c + 1) * B], cond[:, c * P:(c + 1) * P], mem.ident[0:B, 0:B])
            last.then_inc(cond_turned, 1)
            e.wait_ge(rows_loaded, 80)
            e.transpose(bank[3][:, 256:256 + VECS], vec_rows, mem.ident[0:VECS, 0:VECS]).then_inc(rows_turned, 1)
            e.wait_ge(condT_ready, 1)
            for n in range(6):
                e.wait_ge(w_loaded[n], 16)
                if n >= 2:
                    e.wait_ge(ada_ready, n - 1)
                for c in range(DC):
                    last = e.matmul(bank[n % 2][0:B, :], mem.condT[:, c], ada_w[:, c, n * D:(n + 1) * D],
                                    start=(c == 0), stop=(c == DC - 1))
                last.then_inc(ada_done, 1)
            e.wait_ge(ada_ready, 6)
            for i, part in enumerate(PARTS):
                for c in range(DC):
                    at = part * D + c * P
                    last = e.transpose(bank[3][:, (i * DC + c) * B:(i * DC + c + 1) * B], ada[:, at:at + P],
                                       mem.ident[0:B, 0:B])
            last.then_inc(ada_turned, 1)
            ln_pe(e)
            for k, part in enumerate((2, 5)):
                for b in range(B):
                    if k * B + b >= 2:
                        e.wait_ge(gate_ready, k * B + b - 1)
                    e.matmul(bank[b % 2][:, :], mem.sel[:, b, :], ada[:, part * D:(part + 1) * D],
                             start=True, stop=True).then_inc(gate_done, 1)

        @block.vector
        def _(e):
            e.wait_ge(cond_turned, 1)
            e.tensor_copy(mem.condT[:, :, :].rearrange("p c b -> p (c b)"), turned_bank[:, 0:DC * B]).then_inc(condT_ready, 1)
            e.wait_ge(rows_turned, 1)
            e.tensor_copy(mem.vecT[:, :], bank[3][:, 256:256 + VECS]).then_inc(mem.vecT_ready, 1)
            e.wait_ge(adab_loaded, 16)
            for n in range(6):
                e.wait_ge(ada_done, n + 1)
                e.tensor_tensor(ada[:, n * D:(n + 1) * D], bank[n % 2][0:B, :], ada_b[:, n * D:(n + 1) * D],
                                ALU.add).then_inc(ada_ready, 1)
            e.wait_ge(ada_turned, 1)
            for i in range(4):
                part = bank[3][:, i * DC * B:(i + 1) * DC * B]
                e.tensor_scalar(mem.adaT[:, i].rearrange("p c b -> p (c b)"), part, float(i % 2), None,
                                ALU.add).then_inc(adaT_ready, 1)
            ln_dve(e, lambda e, b: e.wait_ge(x_loaded[b], 16))


def attention(nc, mem, a):
    UNITS = 2 * B
    at = [0]

    def place(*shape):
        n = 1
        for k in shape:
            n *= k
        at[0] += n
        return mem.cut(at[0] - n, list(shape))

    def parts(name, *shape):
        got = []
        for part in ("hi", "lo"):
            got.append(mem.rounded(f"{name}_{part}", mem.work, at[0], list(shape)))
            place(*shape)
        return got

    q, k = parts("q", T), parts("k", T)
    v_raw = place(T)
    v = parts("v", TC * DH)
    probs = place(TC, T)
    probsT = parts("probsT", TC, T)
    oT = parts("oT", T)
    scale = place(DC, DH)
    ones = place(DC * 3 * DH)
    assert at[0] <= 13952
    WN = DC * 3 * DH
    w_hi, w_lo = ([mem.rounded(f"w_{part}{i}", mem.work, 13952 + (2 * h + i) * WN, [WN]) for i in range(2)]
                  for h, part in enumerate(("hi", "lo")))
    ow_hi, ow_lo = ([mem.rounded(f"ow_{part}{i}", mem.work, 20096 + (2 * h + i) * D, [D]) for i in range(2)]
                    for h, part in enumerate(("hi", "lo")))
    w_raw = [mem.cut(13952 + (2 + i) * WN, [WN]) for i in range(2)]
    ow_raw = [mem.cut(20096 + (2 + i) * D, [D]) for i in range(2)]
    feat_hi = mem.rounded("feat_hi", mem.tok, 0, [DC, B, T])
    feat_lo = mem.rounded("feat_lo", mem.feat, 0, [DC, B, T])
    pair_bias = mem.small[:, 16:22].rearrange("p (t i) -> p t i", t=3)
    nmax, rinv = mem.small[:, 0:TC], mem.small[:, 4:4 + TC]
    rsum = [mem.small[:, 8 + TC * n:8 + TC * (n + 1)] for n in range(2)]

    def chunk(w, c, t):
        return w[:, :].rearrange("p (k t d) -> p k t d", k=DC, t=3)[:, c, t]

    with ExitStack() as ctx:
        def sem(name):
            return ctx.enter_context(nc.semaphore(name))

        w_loaded = [sem(f"head_loaded{i}") for i in range(2)]
        scale_set, w_scaled, w_rounded = sem("scale_set"), sem("w_scaled"), sem("w_rounded")
        w_split = [sem(f"head_split{i}") for i in range(2)]
        feat_rounded, x_reloaded = sem("feat_rounded"), mem.x_reloaded
        feat_split = [sem(f"feat_split{b}") for b in range(B)]
        acc_done, bias_scaled, bias_ready = sem("acc_done"), sem("bias_scaled"), sem("bias_ready")
        qkv_done, qk_hi, qkv_ready = sem("qkv_done"), sem("qk_hi"), sem("qkv_ready")
        score_done, max_ready, exp_ready, inv_ready = (
            sem(n) for n in ("score_done", "max_ready", "exp_ready", "inv_ready"))
        v_turned, v_hi, v_ready, p_turned, pT_hi, pT_ready = (
            sem(n) for n in ("v_turned", "v_hi", "v_ready", "p_turned", "pT_hi", "pT_ready"))
        o_done, oT_hi, oT_ready, proj_done = sem("o_done"), sem("oT_hi"), sem("oT_ready"), sem("proj_done")
        bank_qkv, bank_s, bank_o = mem.psum[0:2], mem.psum[2:4], mem.psum[6:8]
        turned_bank = [mem.psum[5], mem.psum[4]] + bank_s
        block = ctx.enter_context(nc.Block())
        PAIRS = HEADS // 2

        @block.sync
        def _(e):
            wq = a["qkv_w"].rearrange("(k p) (t h d) -> h p k t d", p=P, t=3, h=HEADS)
            wo = a["out_w"].rearrange("(h d) n -> h d n", h=HEADS)

            def load(i, head):
                into = w_raw[i].rearrange("p (k t d) -> p k t d", k=DC, t=3)
                for t in range(3):
                    e.dma_start(into[:, :, t], wq[head][:, :, t]).then_inc(w_loaded[i], 16)
                e.dma_start(ow_raw[i], wo[head]).then_inc(w_loaded[i], 16)

            for i in range(2):
                load(i, i)
            with e.Fori(0, PAIRS - 1) as g:
                for i in range(2):
                    e.wait_ge(acc_done, (UNITS * g + B * (i + 1)) * TC)
                    load(i, 2 * g + 2 + i)
            e.wait_ge(qkv_done, 3 * UNITS * PAIRS)
            x = a["x"].rearrange("b (t p) d -> b p t d", p=P)
            for b in range(B):
                e.dma_start(mem.tok[:, b * TC:(b + 1) * TC], x[b]).then_inc(x_reloaded[b], 16)
            w1 = mem.cut(13952, [DC, MLP])
            from_w1 = a["ffn_w1"].rearrange("(c p) n -> p c n", p=P)
            e.dma_start(w1[:, 0:DC - 1], from_w1[:, 0:DC - 1]).then_inc(mem.w1_loaded, 16)
            e.wait_ge(proj_done, TC * UNITS * PAIRS)
            e.dma_start(w1[:, DC - 1], from_w1[:, DC - 1]).then_inc(mem.w1_loaded, 16)

        @block.gpsimd
        def _(e):
            def split(i, count, g):
                e.wait_ge(w_loaded[i], 64 * (g + 1))
                wq = w_raw[i].rearrange("p (k t d) -> p k t d", k=DC, t=3)[:, :, 0]
                e.tensor_tensor(wq, wq, scale, ALU.mult).then_inc(w_scaled, 1)
                e.wait_ge(w_scaled, count + 1)
                e.tensor_tensor(w_hi[i][:, :], w_raw[i], ones, ALU.mult).then_inc(w_rounded, 1)
                e.tensor_tensor(ow_hi[i][:, :], ow_raw[i], ones[:, 0:D], ALU.mult).then_inc(w_rounded, 1)
                e.wait_ge(w_rounded, 2 * count + 2)
                e.tensor_tensor(w_lo[i][:, :], w_raw[i], w_hi[i][:, :], ALU.subtract).then_inc(w_split[i], 1)
                e.tensor_tensor(ow_lo[i][:, :], ow_raw[i], ow_hi[i][:, :], ALU.subtract).then_inc(w_split[i], 1)

            e.memset(scale, QSCALE).then_inc(scale_set, 1)
            e.memset(ones, 1.0).then_inc(scale_set, 1)
            e.wait_ge(scale_set, 2)
            split(0, 0, 0)
            for b in (2, 3):
                e.wait_ge(feat_rounded, b + 1)
                e.tensor_tensor(feat_lo[:, :, b], mem.feat[:, :, b], feat_hi[:, :, b], ALU.subtract).then_inc(feat_split[b], 1)
            split(1, 1, 0)
            with e.Fori(1, PAIRS) as g:
                for i in range(2):
                    split(i, 2 * g + i, g)

        def pe_three(e, out, x, y, start, stop):
            e.matmul(out, x[0], y[0], start=start, stop=False)
            e.matmul(out, x[0], y[1], start=False, stop=False)
            return e.matmul(out, x[1], y[0], start=False, stop=stop)

        def pe_qkv(e, g, u, first):
            i, b, n, pair = (u // B) % 2, u % B, 3 * u, g + u // UNITS
            if b == 0:
                e.wait_ge(w_split[i], 2 * (pair + 1))
            if first and u < B:
                e.wait_ge(feat_split[b], 1)
            for t in range(3):
                m = n + t
                if not (first and m < 2):
                    e.wait_ge(qkv_ready, 3 * UNITS * g + m - 1)
                for c in range(DC):
                    last = pe_three(e, bank_qkv[m % 2][:, :], (chunk(w_hi[i], c, t), chunk(w_lo[i], c, t)),
                                    (feat_hi[:, c, b], feat_lo[:, c, b]), c == 0, c == DC - 1)
                last.then_inc(qkv_done, 1)

        def pe_project(e, g, u, t, first):
            i, U, m = (u // B) % 2, UNITS * g + u, 5 * u + 1 + t
            if t == 0:
                e.wait_ge(oT_ready, U + 1)
                if not first:
                    e.wait_ge(acc_done, TC * U)
            elif t >= 2:
                e.wait_ge(acc_done, TC * U + t - 1)
            tile = slice(t * P, (t + 1) * P)
            pe_three(e, bank_o[m % 2][:, :], (oT[0][:, tile], oT[1][:, tile]), (ow_hi[i][:, :], ow_lo[i][:, :]),
                     True, True).then_inc(proj_done, 1)

        def pe_pair(e, g, first=False, final=False):
            for u in range(UNITS):
                start = first and u == 0
                U = UNITS * g + u
                if start:
                    pe_qkv(e, g, 0, first)
                e.wait_ge(qkv_ready, 3 * U + 2)
                for t in range(TC):
                    if not (start and t < 2):
                        e.wait_ge(exp_ready, TC * U + t - 1)
                    tile = slice(t * P, (t + 1) * P)
                    pe_three(e, bank_s[t % 2][:, :], (q[0][:, tile], q[1][:, tile]), (k[0][:, :], k[1][:, :]), True, True).then_inc(score_done, 1)
                    if t == 1:
                        e.wait_ge(qkv_ready, 3 * U + 3)
                        if not start:
                            e.wait_ge(pT_ready, TC * U)
                        for s in range(TC):
                            last = e.transpose(turned_bank[1][:, s * P:(s + 1) * P], v_raw[:, s * P:(s + 1) * P], mem.ident[:, :])
                        last.then_inc(v_turned, 1)
                    if t % 2 == 1 and not start:
                        for n in (t - 1, t):
                            pe_project(e, g, u - 1, n, first and u == 1)
                if not (final and u == UNITS - 1):
                    pe_qkv(e, g, u + 1, first)
                e.wait_ge(exp_ready, TC * U + TC)
                for s in range(TC):
                    if s == 1:
                        e.wait_ge(v_ready, U + 1)
                    for t in range(TC):
                        last = e.transpose(turned_bank[s][:, t * P:(t + 1) * P], probs[:, t, s * P:(s + 1) * P],
                                           mem.ident[:, :])
                    last.then_inc(p_turned, 1)
                if not start:
                    e.wait_ge(acc_done, TC * U - 1)
                for s in range(TC):
                    e.wait_ge(pT_ready, TC * U + s + 1)
                    keys = slice(s * DH, (s + 1) * DH)
                    last = pe_three(e, bank_o[(5 * u) % 2][:, :], (v[0][:, keys], v[1][:, keys]),
                                    (probsT[0][:, s], probsT[1][:, s]), s == 0, s == TC - 1)
                last.then_inc(o_done, 1)
            if final:
                for t in range(TC):
                    pe_project(e, g, UNITS - 1, t, False)

        @block.tensor
        def _(e):
            pe_pair(e, 0, first=True)
            with e.Fori(1, PAIRS - 1) as g:
                pe_pair(e, g)
            pe_pair(e, PAIRS - 1, final=True)

        def act_qkv(e, g, u):
            i, U = (u // B) % 2, UNITS * g + u
            if u % B == 0:
                e.wait_ge(bias_ready, 2 * g + u // B + 1)
            for t in range(2):
                e.wait_ge(qkv_done, 3 * U + t + 1)
                e.activation((q, k)[t][0][:, :], bank_qkv[(3 * u + t) % 2][:, :], ACT.Identity,
                             bias=pair_bias[:, t, i:i + 1]).then_inc(qk_hi, 1)
            e.wait_ge(qkv_done, 3 * U + 3)
            e.wait_ge(qkv_ready, 3 * U + 2)
            e.activation(v_raw, bank_qkv[(3 * u + 2) % 2][:, :], ACT.Identity,
                         bias=pair_bias[:, 2, i:i + 1]).then_inc(qkv_ready, 1)

        def act_pair(e, g, first=False, final=False):
            for u in range(UNITS):
                U = UNITS * g + u
                start = first and u == 0
                if start:
                    act_qkv(e, g, 0)
                for t in range(TC):
                    e.wait_ge(max_ready, TC * U + t + 1)
                    if t == 0 and not start:
                        e.wait_ge(p_turned, TC * U)
                        if not (first and u == 1):
                            e.wait_ge(inv_ready, U - 1)
                    e.activation(probs[:, t], bank_s[t % 2][:, :], ACT.Exp, bias=nmax[:, t:t + 1],
                                 accum_out=rsum[u % 2][:, t:t + 1]).then_inc(exp_ready, 1)
                e.wait_ge(v_turned, U + 1)
                if not start:
                    e.wait_ge(o_done, U)
                e.activation(v[0][:, :], turned_bank[1][:, :], ACT.Copy).then_inc(v_hi, 1)
                if not (final and u == UNITS - 1):
                    act_qkv(e, g, u + 1)
                for s in range(TC):
                    e.wait_ge(p_turned, TC * U + s + 1)
                    e.activation(probsT[0][:, s], turned_bank[s][:, :], ACT.Copy).then_inc(pT_hi, 1)
                e.wait_ge(o_done, U + 1)
                if not start:
                    e.wait_ge(proj_done, TC * U)
                e.activation(oT[0][:, :], bank_o[(5 * u) % 2][:, :], ACT.Copy).then_inc(oT_hi, 1)

        @block.scalar
        def _(e):
            e.preload_act_table(ACT.Exp)
            for b in range(B):
                e.activation(feat_hi[:, :, b], mem.feat[:, :, b], ACT.Copy).then_inc(feat_rounded, 1)
            act_pair(e, 0, first=True)
            with e.Fori(1, PAIRS - 1) as g:
                act_pair(e, g)
            act_pair(e, PAIRS - 1, final=True)

        def dve_rest(e, out, bank, hi):
            return e.tensor_tensor(out, bank[:, :], hi, ALU.subtract)

        def dve_qk(e, g, u):
            i, U = (u // B) % 2, UNITS * g + u
            for t in range(2):
                e.wait_ge(qk_hi, 2 * U + t + 1)
                hi, lo = (q, k)[t]
                e.scalar_tensor_tensor(out=lo[:, :], in0=bank_qkv[(3 * u + t) % 2][:, :], scalar=pair_bias[:, t, i:i + 1],
                                       in1=hi[:, :], op0=ALU.add, op1=ALU.subtract).then_inc(qkv_ready, 1)
                if t == 0:
                    e.wait_ge(qkv_ready, 3 * U + 1)

        def dve_bias(e, i, head):
            e.tensor_scalar(pair_bias[:, :, i:i + 1], mem.qkv_bT[:, :, bass.ds(head, 1)], 0.0, None, ALU.add).then_inc(bias_ready, 1)

        def dve_project(e, g, u, tiles, first):
            b, U = u % B, UNITS * g + u
            for t in tiles:
                e.wait_ge(proj_done, TC * U + t + 1)
                tile = mem.acc[:, b * TC + t]
                e.scalar_tensor_tensor(out=tile, in0=bank_o[(5 * u + 1 + t) % 2][:, :], scalar=rinv[:, t:t + 1],
                                       in1=mem.out_b[:, :] if first and u < B else tile,
                                       op0=ALU.mult, op1=ALU.add).then_inc(acc_done, 1)

        def dve_pair(e, g, first=False, final=False):
            for u in range(UNITS):
                U = UNITS * g + u
                start = first and u == 0
                if start:
                    dve_qk(e, g, 0)
                for t in range(TC):
                    e.wait_ge(score_done, TC * U + t + 1)
                    if t == 0 and not start:
                        e.wait_ge(exp_ready, TC * U)
                    e.tensor_reduce(nmax[:, t:t + 1], bank_s[t % 2][:, :], AX.X, ALU.max, negate=True).then_inc(max_ready, 1)
                    if t % 2 == 1 and not start:
                        dve_project(e, g, u - 1, (t - 1, t), first)
                e.wait_ge(exp_ready, TC * U + TC)
                if not start:
                    e.wait_ge(acc_done, TC * U)
                e.reciprocal(rinv, rsum[u % 2]).then_inc(inv_ready, 1)
                e.wait_ge(inv_ready, U + 1)
                if u == 0:
                    if not first:
                        e.wait_ge(qkv_ready, 3 * U)
                        dve_bias(e, 1, 2 * g + 1)
                elif u == B and not final:
                    e.wait_ge(qkv_ready, 3 * U)
                    dve_bias(e, 0, 2 * g + 2)
                e.wait_ge(v_hi, U + 1)
                dve_rest(e, v[1][:, :], turned_bank[1], v[0][:, :]).then_inc(v_ready, 1)
                if not (final and u == UNITS - 1):
                    dve_qk(e, g, u + 1)
                for s in range(TC):
                    e.wait_ge(pT_hi, TC * U + s + 1)
                    dve_rest(e, probsT[1][:, s], turned_bank[s], probsT[0][:, s]).then_inc(pT_ready, 1)
                e.wait_ge(oT_hi, U + 1)
                dve_rest(e, oT[1][:, :], bank_o[(5 * u) % 2], oT[0][:, :]).then_inc(oT_ready, 1)
            if final:
                dve_project(e, g, UNITS - 1, range(TC), first)

        @block.vector
        def _(e):
            for b in (0, 1):
                e.wait_ge(feat_rounded, b + 1)
                e.tensor_tensor(feat_lo[:, :, b], mem.feat[:, :, b], feat_hi[:, :, b], ALU.subtract).then_inc(feat_split[b], 1)
            e.tensor_scalar(mem.qkv_bT[:, 0], mem.qkv_bT[:, 0], QSCALE, None, ALU.mult).then_inc(bias_scaled, 1)
            e.wait_ge(bias_scaled, 1)
            for i in range(2):
                dve_bias(e, i, i)
            e.wait_ge(bias_ready, 2)
            e.wait_ge(mem.vec_loaded, 32)
            dve_pair(e, 0, first=True)
            with e.Fori(1, PAIRS - 1) as g:
                dve_pair(e, g)
            dve_pair(e, PAIRS - 1, final=True)


def feed_forward(nc, mem, a):
    w1 = mem.cut(13952, [DC, MLP])
    w2 = mem.cut(0, [MC, D])
    hT = [mem.cut(8192 + i * T, [T]) for i in range(2)]
    norm = mem.work[:, 9216:9216 + 2 * TC * D].rearrange("p (r t d) -> p r t d", r=2, t=TC)
    ffn = [mem.cut(9216 + i * D, [D]) for i in range(TC)]
    with ExitStack() as ctx:
        def sem(name):
            return ctx.enter_context(nc.semaphore(name))

        w2_loaded, gated, resid = sem("w2_loaded"), sem("gated"), sem("resid")
        h_done, hT_ready, y_done, y_out, gated_ffn, x_added = (
            sem(n) for n in ("h_done", "hT_ready", "y_done", "y_out", "gated_ffn", "x_added"))
        ffn_added = sem("ffn_added")
        ln_dve, ln_act, ln_pe, turned, act_out, dve_out = layernorm_engines(nc, ctx, mem, "ln2", mem.acc, 2, norm, lambda e: None)
        bank_h, bank_y = mem.psum[0:2], mem.psum[4:8]
        block = ctx.enter_context(nc.Block())

        @block.sync
        def _(e):
            e.dma_start(w2, a["ffn_w2"].rearrange("(c p) n -> p c n", p=P)).then_inc(w2_loaded, 16)

        @block.gpsimd
        def _(e):
            for t in range(NTILE):
                e.wait_ge(resid, t + 1)
                e.tensor_tensor(mem.tok[:, t], mem.tok[:, t], mem.acc[:, t], ALU.add).then_inc(x_added, 1)

        @block.tensor
        def _(e):
            ln_pe(e)
            e.wait_ge(mem.w1_loaded, 32)
            e.wait_ge(w2_loaded, 16)
            e.wait_ge(act_out, 2 * B)
            e.wait_ge(dve_out, 2 * B)
            def batch(b):
                def hidden(m):
                    if m >= 2:
                        e.wait_ge(hT_ready, MC * b + m - 1)
                    for c in range(DC):
                        last = e.matmul(bank_h[m % 2][:, :], w1[:, c, m * P:(m + 1) * P],
                                        mem.feat[:, c, bass.ds(b, 1)].rearrange("p o t -> p (o t)"),
                                        start=(c == 0), stop=(c == DC - 1))
                    last.then_inc(h_done, 1)

                hidden(0)
                for m in range(MC):
                    if m + 1 < MC:
                        hidden(m + 1)
                    e.wait_ge(hT_ready, MC * b + m + 1)
                    for t in range(TC):
                        if m == 0 and t == 0 and not isinstance(b, int):
                            e.wait_ge(y_out, TC * b)
                        last = e.matmul(bank_y[t][:, :], hT[m % 2][:, t * P:(t + 1) * P], w2[:, m],
                                        start=(m == 0), stop=(m == MC - 1))
                    last.then_inc(y_done, 1)

            batch(0)
            with e.Fori(1, B) as b:
                batch(b)

        @block.scalar
        def _(e):
            ln_act(e)
            e.preload_act_table(ACT.Gelu)
            with e.Fori(0, B) as b:
                for m in range(MC):
                    e.wait_ge(h_done, MC * b + m + 1)
                    if m >= 2:
                        e.wait_ge(y_done, MC * b + m - 1)
                    e.activation(hT[m % 2], bank_h[m % 2][:, :], ACT.Gelu, bias=mem.b1T[:, m:m + 1]).then_inc(hT_ready, 1)

        @block.vector
        def _(e):
            def gate_residual(e, b):
                for t in range(b * TC, (b + 1) * TC):
                    e.tensor_tensor(mem.acc[:, t], mem.acc[:, t], mem.gate[:, 0, b], ALU.mult).then_inc(gated, 1)
                e.wait_ge(mem.x_reloaded[b], 16)
                for t in range(b * TC, (b + 1) * TC):
                    e.wait_ge(gated, t + 1)
                    e.tensor_tensor(mem.acc[:, t], mem.acc[:, t], mem.tok[:, t], ALU.add).then_inc(resid, 1)
                e.wait_ge(resid, (b + 1) * TC)

            ln_dve(e, gate_residual)
            e.wait_ge(turned, DC * B)
            e.wait_ge(x_added, NTILE)
            def batch(b):
                e.wait_ge(y_done, MC * b + MC)
                if not isinstance(b, int):
                    e.wait_ge(ffn_added, TC * b)
                for t in range(TC):
                    e.tensor_tensor(ffn[t], bank_y[t][:, :], mem.b2[:, :], ALU.add).then_inc(y_out, 1)
                gate = mem.gate[:, 1, bass.ds(b, 1)].rearrange("p o d -> p (o d)")
                for t in range(TC):
                    e.wait_ge(y_out, TC * b + t + 1)
                    e.tensor_tensor(ffn[t], ffn[t], gate, ALU.mult).then_inc(gated_ffn, 1)
                for t in range(TC):
                    e.wait_ge(gated_ffn, TC * b + t + 1)
                    tile = mem.tok[:, bass.ds(TC * b + t, 1)].rearrange("p o d -> p (o d)")
                    e.tensor_tensor(tile, tile, ffn[t], ALU.add).then_inc(ffn_added, 1)

            batch(0)
            with e.Fori(1, B) as b:
                batch(b)


def convolution(nc, mem, a):
    coupling = mem.cut(0, [DC, D])
    couplingT = mem.cut(2048, [DC, D])
    with ExitStack() as ctx:
        def sem(name):
            return ctx.enter_context(nc.semaphore(name))

        turned, copied, tap, tap1 = sem("x_turned"), sem("x_copied"), sem("tap"), sem("tap_first")
        c_turned = sem("coupling_turned")
        bank = mem.psum[0:4]
        block = ctx.enter_context(nc.Block())

        @block.sync
        def _(e):
            e.dma_start(coupling, a["coupling"].rearrange("(c p) n -> p c n", p=P)).then_inc(mem.coupling_loaded, 16)

        @block.tensor
        def _(e):
            n = 0
            for b in range(B):
                for c in range(DC):
                    if n >= 4:
                        e.wait_ge(tap, n - 3)
                    for t in range(TC):
                        last = e.transpose(bank[n % 4][:, t * P:(t + 1) * P], mem.tok[:, b * TC + t, c * P:(c + 1) * P],
                                           mem.ident[:, :])
                    last.then_inc(turned, 1)
                    n += 1
            e.wait_ge(mem.coupling_loaded, 16)
            for c in range(DC):
                for r in range(DC):
                    last = e.transpose(mem.psum[4 + c][:, r * P:(r + 1) * P], coupling[:, r, c * P:(c + 1) * P],
                                       mem.ident[:, :])
                last.then_inc(c_turned, 1)

        @block.scalar
        def _(e):
            for n in range(B * DC):
                b, c = n // DC, n % DC
                e.wait_ge(turned, n + 1)
                e.activation(mem.feat[:, c, b], bank[n % 4][:, :], ACT.Identity,
                             bias=mem.convbT[:, c:c + 1]).then_inc(copied, 1)
            for c in range(DC):
                e.wait_ge(c_turned, c + 1)
                e.activation(couplingT[:, c], mem.psum[4 + c][:, :], ACT.Copy).then_inc(copied, 1)

        @block.vector
        def _(e):
            for n in range(B * DC):
                b, c = n // DC, n % DC
                x = bank[n % 4]
                e.wait_ge(copied, n + 1)
                for back in range(B):
                    if back:
                        e.wait_ge(tap1, n * (B - 1) + back)
                    out = mem.feat[:, c, b, back:]
                    e.scalar_tensor_tensor(out=out, in0=x[:, 0:T - back], scalar=mem.condT[:, c, B - 1 - back:B - back],
                                           in1=out, op0=ALU.mult, op1=ALU.add).then_inc(tap if back == B - 1 else tap1, 1)



def coupled_scan(nc, mem, a):
    N = DC * B
    QT = P // 4
    couplingT = mem.cut(2048, [DC, D])
    at = [4096]

    def state(n=N):
        at[0] += n
        return mem.cut(at[0] - n, [n])

    q, q2, q3, q4, q_new = (state() for _ in range(5))
    p, p2, p3, p4, p_new = (state() for _ in range(5))
    v = [state() for _ in range(4)]
    dq = [state() for _ in range(3)]
    square, cubic, drive, bias, dq_sum, v_mid, v_ends, v_sum, lessp0, lessp, lead_dq = (
        state() for _ in range(11))
    lead, base, partial = ([state() for _ in range(2)] for _ in range(3))
    tanh_q = state()
    back = [state(P) for _ in range(2)]
    idle = mem.cut(at[0], [P]).bitcast(BF16)[:, 0:P]
    x = mem.feat[:, :, :, :].rearrange("p c b t -> p (c b) t")
    C = [H_STEP / 2, H_STEP / 2, H_STEP, H_STEP / 6]
    Q, PP = [q, q2, q3, q4], [p, p2, p3, p4]
    with ExitStack() as ctx:
        def sem(name):
            return ctx.enter_context(nc.semaphore(name))

        set_up, vec, q_ready, q_clipped, v_ready, p_ready, square_ready, lessp_ready = (
            sem(n) for n in ("scan_set_up", "vec", "q_ready", "q_clipped", "v_ready", "p_ready", "square_ready",
                             "lessp_ready"))
        tanh_ready, m_ready, dq_ready, v_mid_ready, v_ends_ready = (
            sem(n) for n in ("tanh_ready", "m_ready", "dq_ready", "v_mid_ready", "v_ends_ready"))
        STEPS = 6
        assert (T - 2) % STEPS == 0
        block = ctx.enter_context(nc.Block())

        @block.scalar
        def _(e):
            e.preload_act_table(ACT.Tanh)
            with e.Fori(0, T) as t:
                for i in range(4):
                    e.wait_ge(q_ready, 4 * t + i + 1)
                    e.activation(tanh_q, Q[i] if i else q_new, ACT.Tanh).then_inc(tanh_ready, 1)

        @block.tensor
        def _(e):
            e.wait_ge(set_up, 4 + B)
            with e.Fori(0, T) as t:
                for i in range(4):
                    e.wait_ge(tanh_ready, 4 * t + i + 1)
                    for c in range(DC):
                        for j in range(4):
                            cols = couplingT[:, c].rearrange("p (s j k) -> p j s k", s=DC, j=4)[:, j]
                            last = e.matmul(mem.psum[i % 2][QT * j:QT * j + B, 0:P], tanh_q[:, B * c:B * c + B], cols,
                                            start=(c == 0), stop=(c == DC - 1), tile_position=(0, QT * j))
                    last.then_inc(m_ready, 1)
                    for _ in range(KEEP_WARM):
                        e.matmul(mem.psum[2][:, 0:P], idle, idle, start=True, stop=True)

        @block.gpsimd
        def _(e):
            e.wait_ge(set_up, 5 + B)
            with e.Fori(0, T) as t:
                for i in range(4):
                    if i == 0:
                        e.wait_ge(q_clipped, t + 1)
                    else:
                        e.wait_ge(q_ready, 4 * t + i + 1)
                    e.tensor_tensor(square, Q[i], Q[i], ALU.mult).then_inc(square_ready, 1)
                    if i < 3:
                        e.wait_ge(p_ready, 3 * t + i + 1)
                        e.tensor_tensor(lessp, drive, PP[i + 1], ALU.subtract).then_inc(lessp_ready, 1)
                    if i > 0:
                        e.tensor_tensor(dq[i - 1], Q[i], q, ALU.subtract).then_inc(dq_ready, 1)
                    if i == 2:
                        e.wait_ge(v_ready, 4 * t + 3)
                        e.tensor_tensor(v_mid, v[1], v[2], ALU.add).then_inc(v_mid_ready, 1)
                    if i == 3:
                        e.wait_ge(v_ready, 4 * t + 4)
                        e.tensor_tensor(v_ends, v[0], v[3], ALU.add).then_inc(v_ends_ready, 1)

        @block.vector
        def _(e):
            e.memset(mem.psum[0][:, 0:P], 0.0).then_inc(set_up, 1)
            e.memset(mem.psum[1][:, 0:P], 0.0).then_inc(set_up, 1)
            e.memset(idle, 0.0).then_inc(set_up, 1)
            cond = mem.condT[:, :, :].rearrange("p c b -> p (c b)")
            e.tensor_scalar(p, cond, -P_SHIFT, None, ALU.add).then_inc(set_up, 1)
            for b in range(B):
                e.tensor_scalar(bias.rearrange("p (c b) -> p c b", b=B)[:, :, b], mem.cbiasT, -P_SHIFT, None,
                                ALU.add).then_inc(set_up, 1)
            e.wait_ge(set_up, 4 + B)
            e.tensor_copy(q_new, cond).then_inc(q_ready, 1)
            e.tensor_tensor(drive, x[:, :, 0], bias, ALU.add).then_inc(set_up, 1)
            e.tensor_copy(q, cond).then_inc(q_clipped, 1)
            e.wait_ge(set_up, 5 + B)
            e.wait_ge(q_clipped, 1)
            OPS = 29

            def fma(out, in0, scalar, in1, op1=ALU.add):
                return e.scalar_tensor_tensor(out=out, in0=in0, scalar=scalar, in1=in1, op0=ALU.mult, op1=op1)

            def x_at(t):
                return x[:, :, bass.ds(t, 1)].rearrange("p n o -> p (n o)")

            def step(t, first=False, last=False):
                before = 0 if first else OPS * t - 1
                done = {}
                count = [0]

                def signal(name, instruction):
                    count[0] += 1
                    done[name] = count[0]
                    instruction.then_inc(vec, 1)

                def need(*names):
                    e.wait_ge(vec, before + max(done[n] for n in names))

                for i in range(4):
                    qi, pi, c, even = Q[i], PP[i], C[i], i % 2
                    fma(v[i], pi, -BETA, qi).then_inc(v_ready, 1)
                    if i == 0:
                        signal("lessp0", e.tensor_tensor(lessp0, drive, p, ALU.subtract))
                    if i < 3:
                        e.wait_ge(v_ready, 4 * t + i + 1)
                        fma(PP[i + 1], v[i], c * EPSILON, p).then_inc(p_ready, 1)
                    if i == 0:
                        need("lessp0")
                        signal("lead0", fma(lead[0], lessp0, c, q))
                    e.wait_ge(square_ready, 4 * t + i + 1)
                    signal("cubic", fma(cubic, square, -1 / 3, qi, ALU.mult))
                    if i < 3:
                        need(f"lead{i}")
                        signal("partial", fma(partial[even], qi, c, lead[even]))
                    if i == 1 and not first:
                        signal("trace", e.tensor_tensor(x_at(t - 1), x_at(t - 1), q, ALU.add))
                    if i < 3:
                        need("partial", "cubic")
                        signal("base", fma(base[even], cubic, c, partial[even]))
                        e.wait_ge(lessp_ready, 3 * t + i + 1)
                        signal(f"lead{i + 1}", fma(lead[1 - even], lessp, C[i + 1], q))
                    if i == 2:
                        e.wait_ge(dq_ready, 3 * t + 2)
                        signal("dq_sum", fma(dq_sum, dq[1], 2.0, dq[0]))
                        need("dq_sum", "lead3")
                        signal("lead_dq", fma(lead_dq, dq_sum, 1 / 3, lead[1]))
                    if i == 3:
                        need("lead_dq")
                        signal("partial3", fma(partial[0], qi, c, lead_dq))
                        if not last:
                            signal("drive", e.tensor_tensor(drive, x_at(t + 1), bias, ALU.add))
                        need("partial3", "cubic")
                        signal("partial", fma(partial[1], cubic, c, partial[0]))
                        e.wait_ge(v_mid_ready, t + 1)
                        e.wait_ge(v_ends_ready, t + 1)
                        signal("v_sum", fma(v_sum, v_mid, 2.0, v_ends))
                        need("partial")
                        e.wait_ge(dq_ready, 3 * t + 3)
                        signal("base", fma(base[1], dq[2], 1 / 3, partial[1]))
                        need("v_sum")
                        signal("p_new", fma(p_new, v_sum, C[3] * EPSILON, p))
                        need("p_new")
                        signal("p", e.tensor_scalar(p, p_new, CLAMP - P_SHIFT, -CLAMP - P_SHIFT, ALU.min, ALU.max))
                    e.wait_ge(m_ready, 4 * t + i + 1)
                    signal("back", e.transpose(back[even], mem.psum[even][:, 0:P]))
                    need("back", "base")
                    coupled = back[even].rearrange("p (c r) -> p c r", c=DC)[:, :, 0:B]
                    to = Q[i + 1] if i < 3 else q_new
                    fma(to.rearrange("p (c b) -> p c b", c=DC), coupled, c,
                        base[even].rearrange("p (c b) -> p c b", c=DC)).then_inc(q_ready, 1)
                    e.wait_ge(q_ready, 4 * t + i + 2)
                e.tensor_scalar(q, q_new, CLAMP, -CLAMP, ALU.min, ALU.max).then_inc(q_clipped, 1)
                e.wait_ge(q_clipped, t + 2)
                assert last or count[0] == OPS - first, count

            step(0, first=True)
            with e.Fori(0, (T - 2) // STEPS) as k:
                for n in range(STEPS):
                    step(k * STEPS + (1 + n))
            step(T - 1, last=True)
            e.tensor_tensor(x_at(T - 1), x_at(T - 1), q, ALU.add).then_inc(vec, 1)


def top_k(nc, mem, a):
    at = [0]

    def place(*shape):
        n = 1
        for k in shape:
            n *= k
        at[0] += n
        return mem.cut(at[0] - n, list(shape))

    ones, before = place(P), place(P)
    eq, rank, one_row = place(NTILE, D), place(2, D), place(D)
    nmax, rsum, rinv = place(NTILE), place(NTILE), place(NTILE)
    count, bit_value, left = (place(B) for _ in range(3))
    candidate, found, bit, taken, next_bit = (place(B).bitcast(I32) for _ in range(5))
    ones16 = place(P).bitcast(BF16)[:, 0:P]
    unused = [place(D) for _ in range(B)]
    mask = [mem.cut(2 * P + b * TC * D // 2, [TC * D // 2]).bitcast(BF16) for b in range(B)]
    row_count, row_before, offset = place(NTILE), place(NTILE), place(NTILE)
    emb_t = mem.gate[:, 0]
    with ExitStack() as ctx:
        def sem(name):
            return ctx.enter_context(nc.semaphore(name))

        emb_loaded, const, turned, copied, max_ready, exp_ready, inv_ready, soft, prod, adj_ready = (
            sem(n) for n in ("emb_loaded", "topk_const", "x4_turned", "x4_copied", "row_max", "row_exp", "row_inv",
                             "row_soft", "adj_product", "adj_ready"))
        mask_ready, summed, counted, chosen = sem("mask_ready"), sem("summed"), sem("counted"), sem("chosen")
        tie, tie_sum, ranked, picked, masked, stored = (
            sem(n) for n in ("tie", "tie_sum", "ranked", "picked", "masked", "stored"))
        bank = mem.psum[0:4]
        block = ctx.enter_context(nc.Block())
        BITS = 31
        STEPS = BITS + 2

        @block.sync
        def _(e):
            for b in range(B):
                e.dma_start(emb_t[:, b], a["cond"][b:b + 1].broadcast_to((P, D))).then_inc(emb_loaded, 16)
            y = a["out"].rearrange("b (t p) d -> b p t d", p=P)
            for b in range(B):
                e.wait_ge(masked, TC * (b + 1))
                e.dma_start(y[b], mem.tok[:, b * TC:(b + 1) * TC]).then_inc(stored, 16)
            e.wait_ge(stored, 16 * B)

        @block.gpsimd
        def _(e):
            e.memset(ones, 1.0).then_inc(const, 1)
            e.memset(ones16, 1.0).then_inc(const, 1)
            e.memset(before, 1.0).then_inc(const, 1)
            e.wait_ge(const, 3)
            e.affine_select(out=before, in_=before, compare_op=ALU.is_gt, fill=0.0, base=0,
                            pattern=[[1, P]], channel_multiplier=-1).then_inc(const, 1)
            for n in range(NTILE):
                t = n % TC
                e.wait_ge(prod, n + 1)
                diag = mem.acc[:, n, t * P:(t + 1) * P]
                e.affine_select(out=diag, in_=diag, compare_op=ALU.not_equal, fill=-3.0e38, base=0,
                                pattern=[[-1, P]], channel_multiplier=1).then_inc(adj_ready, 1)
            for n in range(NTILE):
                e.wait_ge(picked, n + 1)
                e.tensor_tensor(mem.tok[:, n], mem.tok[:, n], eq[:, n], ALU.add).then_inc(masked, 1)

        @block.tensor
        def _(e):
            for n in range(NTILE):
                b, t = n // TC, n % TC
                if n >= 4:
                    e.wait_ge(copied, n - 3)
                for c in range(DC):
                    last = e.transpose(bank[n % 4][:, c * P:(c + 1) * P], mem.feat[:, c, b, t * P:(t + 1) * P],
                                       mem.ident[:, :])
                last.then_inc(turned, 1)
            e.wait_ge(const, 4)

            def sum_masks(step, first=False):
                for b in range(B):
                    if not first:
                        e.wait_ge(counted, B * (step - 1) + b + 1)
                    e.wait_ge(mask_ready, B * step + b + 1)
                    for t in range(TC):
                        last = e.matmul(mem.psum[b][:, :], ones16, mask[b][:, t * D:(t + 1) * D],
                                        start=(t == 0), stop=(t == TC - 1))
                    last.then_inc(summed, 1)

            sum_masks(0, first=True)
            with e.Fori(1, STEPS) as step:
                sum_masks(step)
            e.wait_ge(tie, TC - 1)
            e.matmul(mem.psum[5][:, 0:NTILE], before, row_count, start=True, stop=False)
            e.matmul(mem.psum[5][:, 0:NTILE], ones, row_before, start=False, stop=True).then_inc(tie_sum, 1)

        @block.scalar
        def _(e):
            e.preload_act_table(ACT.Exp)
            for n in range(NTILE + 1):
                if n < NTILE:
                    e.wait_ge(turned, n + 1)
                    e.activation(mem.tok[:, n], bank[n % 4][:, :], ACT.Copy).then_inc(copied, 1)
                if n >= 1:
                    e.wait_ge(max_ready, n)
                    e.activation(mem.acc[:, n - 1], mem.tok[:, n - 1], ACT.Exp, bias=nmax[:, n - 1:n],
                                 accum_out=rsum[:, n - 1:n]).then_inc(exp_ready, 1)
            with e.Fori(0, STEPS) as step:
                for b in range(B):
                    e.wait_ge(summed, B * step + b + 1)
                    e.activation(unused[b], mem.psum[b][:, :], ACT.Copy, accum_out=count[:, b:b + 1]).then_inc(counted, 1)

        @block.vector
        def _(e):
            e.wait_ge(emb_loaded, 16 * B)

            def weigh(n):
                b = n // TC
                e.wait_ge(exp_ready, n + 1)
                e.reciprocal(rinv[:, n:n + 1], rsum[:, n:n + 1]).then_inc(inv_ready, 1)
                e.wait_ge(inv_ready, n + 1)
                e.tensor_scalar(mem.acc[:, n], mem.acc[:, n], rinv[:, n:n + 1], T ** -0.5, ALU.mult, ALU.mult).then_inc(soft, 1)
                e.wait_ge(soft, n + 1)
                e.scalar_tensor_tensor(out=mem.acc[:, n], in0=emb_t[:, b], scalar=mem.emb_s[:, n:n + 1],
                                       in1=mem.acc[:, n], op0=ALU.mult, op1=ALU.mult).then_inc(prod, 1)

            for n in range(NTILE):
                e.wait_ge(copied, n + 1)
                e.tensor_reduce(nmax[:, n:n + 1], mem.tok[:, n], AX.X, ALU.max, negate=True).then_inc(max_ready, 1)
                if n >= 1:
                    weigh(n - 1)
            weigh(NTILE - 1)
            steps = [0]

            def chain(instruction):
                instruction.then_inc(chosen, 1)
                steps[0] += 1
                e.wait_ge(chosen, steps[0])

            def compare(b, threshold, how):
                flat = mem.acc[:, b * TC:(b + 1) * TC].rearrange("p t d -> p (t d)")
                e.tensor_scalar(mask[b], flat, threshold, None, how).then_inc(mask_ready, 1)

            def compare_candidate(g):
                for b in (2 * g, 2 * g + 1):
                    compare(b, candidate[:, b:b + 1].bitcast(F32), ALU.is_ge)

            e.wait_ge(adj_ready, NTILE)
            for b in range(B):
                compare(b, 0.0, ALU.is_ge)
            chain(e.memset(one_row, 1.0))
            chain(e.memset(bit, 1 << 30))
            chain(e.memset(bit_value, float(1 << 30)))
            e.wait_ge(counted, B)
            chain(e.tensor_scalar(found, count, float(TOPK), -1.0, ALU.is_lt, ALU.mult))
            chain(e.tensor_tensor(candidate, found, bit, ALU.bitwise_xor))
            for g in range(2):
                compare_candidate(g)
            head = steps[0]
            CHAIN = 10
            with e.Fori(1, BITS) as k:
                done = [0]

                def link(instruction):
                    instruction.then_inc(chosen, 1)
                    done[0] += 1

                def need(n):
                    e.wait_ge(chosen, CHAIN * k + (head - CHAIN) + n)

                link(e.tensor_scalar(bit, bit, 1, None, ALU.logical_shift_right))
                need(1)
                for g in range(2):
                    pair = slice(2 * g, 2 * g + 2)
                    link(e.tensor_tensor(next_bit[:, pair], found[:, pair], bit[:, pair], ALU.bitwise_xor))
                for g in range(2):
                    pair = slice(2 * g, 2 * g + 2)
                    e.wait_ge(counted, B * k + 2 * g + 2)
                    link(e.scalar_tensor_tensor(out=taken[:, pair], in0=count[:, pair], scalar=float(TOPK),
                                                in1=bit_value[:, pair], op0=ALU.is_ge, op1=ALU.mult))
                    need(done[0])
                    link(e.tensor_tensor(candidate[:, pair], next_bit[:, pair], taken[:, pair], ALU.bitwise_xor))
                    link(e.tensor_tensor(found[:, pair], found[:, pair], taken[:, pair], ALU.bitwise_xor))
                    if g == 1:
                        link(e.tensor_scalar(bit_value, bit_value, 0.5, None, ALU.mult))
                        need(done[0])
                    else:
                        need(done[0] - 1)
                    compare_candidate(g)
                assert done[0] == CHAIN
            steps[0] = head + CHAIN * (BITS - 1)
            e.wait_ge(counted, B * (BITS + 1))
            chain(e.scalar_tensor_tensor(out=taken, in0=count, scalar=float(TOPK), in1=bit_value,
                                         op0=ALU.is_ge, op1=ALU.mult))
            chain(e.tensor_tensor(found, found, taken, ALU.bitwise_xor))
            threshold = found.bitcast(F32)
            for b in range(B):
                compare(b, threshold[:, b:b + 1], ALU.is_gt)
            e.wait_ge(counted, B * STEPS)
            chain(e.tensor_scalar(left, count, -1.0, float(TOPK), ALU.mult, ALU.add))
            for n in range(NTILE):
                b = n // TC
                last = e.tensor_scalar(eq[:, n], mem.acc[:, n], threshold[:, b:b + 1], None, ALU.is_equal, ALU.add,
                                       accum_out=row_count[:, n:n + 1])
            chain(last)
            rows, sums = (r.rearrange("p (b t) -> p t b", b=B) for r in (row_count, row_before))
            chain(e.memset(sums[:, 0], 0.0))
            for t in range(1, TC):
                e.tensor_tensor(sums[:, t], sums[:, t - 1], rows[:, t - 1], ALU.add).then_inc(tie, 1)
                e.wait_ge(tie, t)
            e.wait_ge(tie_sum, 1)
            chain(e.tensor_copy(offset, mem.psum[5][:, 0:NTILE]))
            for n in range(NTILE):
                b = n // TC
                e.tensor_tensor_scan(rank[:, n % 2], one_row, eq[:, n], offset[:, n:n + 1], ALU.mult, ALU.add).then_inc(ranked, 1)
                e.wait_ge(ranked, 2 * n + 1)
                e.scalar_tensor_tensor(out=eq[:, n], in0=rank[:, n % 2], scalar=left[:, b:b + 1], in1=eq[:, n],
                                       op0=ALU.is_le, op1=ALU.mult).then_inc(ranked, 1)
                e.wait_ge(ranked, 2 * n + 2)
                e.scalar_tensor_tensor(out=eq[:, n], in0=mem.acc[:, n], scalar=threshold[:, b:b + 1], in1=eq[:, n],
                                       op0=ALU.is_gt, op1=ALU.add).then_inc(picked, 1)


INPUTS = {"x": "x", "cond": "cond_2048", "fside": "fside_BxSx1_0", "ada_w": "L0_cond_ada_w", "ada_b": "L0_cond_ada_b",
          "qkv_w": "L0_cond_qkv_w", "qkv_b": "L0_cond_qkv_b", "out_w": "L0_cond_out_w", "out_b": "L0_cond_out_b",
          "ffn_w1": "L0_cond_ffn_w1", "ffn_b1": "L0_cond_ffn_b1", "ffn_w2": "L0_cond_ffn_w2", "ffn_b2": "L0_cond_ffn_b2",
          "conv_b": "L1_cond_b", "coupling": "L2_cond_coupling", "bias": "L2_cond_bias"}


def program(nc, a):
    with ExitStack() as ctx:
        mem = Memory(nc, ctx)
        prepare(nc, mem, a)
        attention(nc, mem, a)
        feed_forward(nc, mem, a)
        convolution(nc, mem, a)
        coupled_scan(nc, mem, a)
        top_k(nc, mem, a)


def kernel(**inputs):
    import numpy as np
    import concourse.bacc as bacc
    from concourse.bass_utils import run_bass_kernel_spmd

    nc = bacc.Bacc("TRN2", target_bir_lowering=False, num_devices=1)
    arrays, a = {}, {}
    for short, name in INPUTS.items():
        v = np.ascontiguousarray(inputs[name])
        arrays["in_" + name] = v
        a[short] = nc.dram_tensor("in_" + name, v.shape, mybir.dt.from_np(v.dtype), kind="ExternalInput").ap()
    a["out"] = nc.dram_tensor("out", (B, T, D), F32, kind="ExternalOutput").ap()
    program(nc, a)
    r = run_bass_kernel_spmd(nc, [arrays], core_ids=[0])
    return r.results[0]["out"]
```

```python
import concourse.bass as bass
from concourse import mybir
from contextlib import ExitStack

F32 = mybir.dt.float32
I32 = mybir.dt.int32
BF16 = mybir.dt.bfloat16
F32R = mybir.dt.float32r
ACT = mybir.ActivationFunctionType
ALU = mybir.AluOpType
AX = mybir.AxisListType

P = 128
B, T, D = 4, 512, 512
TC, DC = T // P, D // P
NTILE = B * TC
HEADS, DH = 16, 128
INNER = HEADS * DH
MLP = 2048
MC = MLP // P
QSCALE = DH ** -0.5
LN_EPS = 1e-6
TOPK = 5120
H_STEP, EPSILON, ALPHA, BETA, CLAMP = 0.01, 0.08, 0.7, 0.8, 20.0
P_SHIFT = ALPHA / BETA
KEEP_WARM = 4


VECS = MC + NTILE + 2 * DC + 3 * HEADS


class Memory:

    def __init__(self, nc, ctx):
        self.nc, self.ends = nc, {}

        def sb(name, shape, dt=F32):
            tensor = ctx.enter_context(nc.sbuf_tensor(name, shape, dt))
            self.ends[name] = nc.sbuf_base
            return tensor

        self.tok = sb("tok", [P, NTILE, D])
        self.acc = sb("acc", [P, NTILE, D])
        self.feat = sb("feat", [P, DC, B, T])
        self.gate = sb("gate", [P, 2, B, D])
        self.work = sb("work", [P, 22400])
        self.ident = sb("ident", [P, P])
        self.sel = sb("sel", [B, B, P])
        self.condT = sb("condT", [P, DC, B])
        self.adaT = sb("adaT", [P, 4, DC, B])
        self.out_b = sb("out_b", [P, D])
        self.b2 = sb("b2", [P, D])
        self.vecT = sb("vecT", [P, VECS])
        self.b1T = self.vecT[:, 0:MC]
        self.emb_s = self.vecT[:, MC:MC + NTILE]
        self.convbT = self.vecT[:, 32:32 + DC]
        self.cbiasT = self.vecT[:, 36:36 + DC]
        self.qkv_bT = self.vecT[:, 40:40 + 3 * HEADS].rearrange("p (t h) -> p t h", t=3)
        self.stats = sb("stats", [P, NTILE, 6])
        self.mv = sb("mv", [P, NTILE, 2])
        self.rstd = sb("rstd", [P, 2, NTILE])
        self.small = sb("small", [P, 64])
        self.psum = [ctx.enter_context(nc.psum_tensor(f"bank{i}", [P, 512], F32)) for i in range(8)]
        self.const_ready = ctx.enter_context(nc.semaphore("const_ready"))
        self.vec_loaded = ctx.enter_context(nc.semaphore("vec_loaded"))
        self.vecT_ready = ctx.enter_context(nc.semaphore("vecT_ready"))
        self.x_reloaded = [ctx.enter_context(nc.semaphore(f"x_reloaded{b}")) for b in range(B)]
        self.w1_loaded = ctx.enter_context(nc.semaphore("w1_loaded"))
        self.coupling_loaded = ctx.enter_context(nc.semaphore("coupling_loaded"))

    def rounded(self, name, within, start, shape):
        n = 1
        for k in within.shape[1:]:
            n *= k
        first = self.ends[within.name] - 4 * (n - start)
        return self.nc.alloc_sbuf_tensor_at(name, [P] + shape, F32R, offset=first)

    def cut(self, start, shape):
        n = 1
        for s in shape:
            n *= s
        flat = self.work[:, start:start + n]
        if len(shape) == 1:
            return flat
        names = "abc"[:len(shape)]
        return flat.rearrange(f"p ({' '.join(names)}) -> p {' '.join(names)}",
                              **{k: v for k, v in zip(names, shape)})


def layernorm_engines(nc, ctx, mem, block_name, src, shift, norm, cond_ready):
    def sem(name):
        return ctx.enter_context(nc.semaphore(f"{block_name}_{name}"))

    stat, var_ready, std_ready, norm_ready, turned, act_out, dve_out = (
        sem(n) for n in ("stat", "var_ready", "std_ready", "norm_ready", "turned", "act_out", "dve_out"))
    bank = mem.psum[4:8]

    def dve(e, src_ready):
        for b in range(B):
            src_ready(e, b)
            tiles = range(b * TC, (b + 1) * TC)
            for t in tiles:
                e.bn_stats(mem.stats[:, t], src[:, t]).then_inc(stat, 1)
            for n, t in enumerate(tiles):
                e.wait_ge(stat, (2 * b) * TC + n + 1)
                e.bn_aggr(mem.mv[:, t], mem.stats[:, t]).then_inc(stat, 1)
            e.wait_ge(stat, (2 * b + 2) * TC)
            e.tensor_scalar(mem.rstd[:, 0, b * TC:(b + 1) * TC], mem.mv[:, b * TC:(b + 1) * TC, 1],
                            LN_EPS, None, ALU.add).then_inc(var_ready, 1)
            e.wait_ge(std_ready, 2 * b + 1)
            e.reciprocal(mem.rstd[:, 1, b * TC:(b + 1) * TC],
                         mem.rstd[:, 0, b * TC:(b + 1) * TC]).then_inc(std_ready, 1)
            e.wait_ge(std_ready, 2 * b + 2)
            if b >= 2:
                e.wait_ge(turned, DC * (b - 1))
            for n, t in enumerate(tiles):
                e.tensor_scalar(norm[:, b % 2, n], src[:, t], mem.mv[:, t, 0:1],
                                mem.rstd[:, 1, t:t + 1], ALU.subtract, ALU.mult).then_inc(norm_ready, 1)
            cond_ready(e)
            for c in (1, 3):
                e.wait_ge(turned, DC * b + c + 1)
                e.tensor_scalar(mem.feat[:, c, b], bank[c][:, :], mem.adaT[:, shift + 1, c, b:b + 1],
                                mem.adaT[:, shift, c, b:b + 1], ALU.mult, ALU.add).then_inc(dve_out, 1)

    def act(e):
        for b in range(B):
            e.wait_ge(var_ready, b + 1)
            e.activation(mem.rstd[:, 0, b * TC:(b + 1) * TC], mem.rstd[:, 0, b * TC:(b + 1) * TC],
                         ACT.Sqrt).then_inc(std_ready, 1)
            cond_ready(e)
            for c in (0, 2):
                e.wait_ge(turned, DC * b + c + 1)
                e.activation(mem.feat[:, c, b], bank[c][:, :], ACT.Identity,
                             bias=mem.adaT[:, shift, c, b:b + 1],
                             scale=mem.adaT[:, shift + 1, c, b:b + 1]).then_inc(act_out, 1)

    def pe(e):
        for b in range(B):
            e.wait_ge(norm_ready, TC * (b + 1))
            for c in range(DC):
                if b >= 1:
                    e.wait_ge(act_out if c % 2 == 0 else dve_out, 2 * (b - 1) + c // 2 + 1)
                for n in range(TC):
                    last = e.transpose(bank[c][:, n * P:(n + 1) * P], norm[:, b % 2, n, c * P:(c + 1) * P],
                                       mem.ident[:, :])
                last.then_inc(turned, 1)

    return dve, act, pe, turned, act_out, dve_out


def prepare(nc, mem, a):
    ada_w = mem.cut(0, [DC, 6 * D])
    ada = mem.cut(12288, [6 * D])[0:B]
    norm = mem.work[:, 15360:15360 + 2 * TC * D].rearrange("p (r t d) -> p r t d", r=2, t=TC)
    rows = mem.gate[0:B].rearrange("p k b d -> p (k b d)")
    ada_b, cond = rows[:, 0:6 * D], rows[:, 6 * D:7 * D]
    vec_rows = mem.cut(19456, [P])[0:VECS]
    with ExitStack() as ctx:
        def sem(name):
            return ctx.enter_context(nc.semaphore(name))

        x_loaded = [sem(f"x_loaded{b}") for b in range(B)]
        w_loaded = [sem(f"ada_w_loaded{n}") for n in range(6)]
        cond_loaded, adab_loaded, zeroed = sem("cond_loaded"), sem("adab_loaded"), sem("zeroed")
        rows_loaded, rows_turned = sem("rows_loaded"), sem("rows_turned")
        cond_turned, condT_ready = sem("cond_turned"), sem("condT_ready")
        ada_done, ada_ready, ada_turned, adaT_ready = (sem(n) for n in ("ada_done", "ada_ready", "ada_turned", "adaT_ready"))
        gate_done, gate_ready = sem("gate_done"), sem("gate_ready")
        turned_bank, bank = mem.psum[2], mem.psum
        PARTS = (0, 1, 3, 4)

        def cond_ready(e):
            e.wait_ge(adaT_ready, 4)

        ln_dve, ln_act, ln_pe, *_ = layernorm_engines(nc, ctx, mem, "ln1", mem.tok, 0, norm, cond_ready)
        block = ctx.enter_context(nc.Block())

        @block.sync
        def _(e):
            e.dma_start(cond, a["cond"]).then_inc(cond_loaded, 16)
            e.dma_start(ada_b, a["ada_b"].rearrange("(o n) -> o n", o=1).broadcast_to((B, 6 * D))).then_inc(adab_loaded, 16)
            at = 0
            for name in ("ffn_b1", "fside", "conv_b", "bias", "qkv_b"):
                v = a[name].rearrange("b t o -> (b t o)") if name == "fside" else a[name]
                n = v.shape[0] // P
                e.dma_start(vec_rows[at:at + n], v.rearrange("(c p) -> c p", p=P)).then_inc(rows_loaded, 16)
                at += n
            w = a["ada_w"].rearrange("(c p) n -> p c n", p=P)
            x = a["x"].rearrange("b (t p) d -> b p t d", p=P)
            for n in range(6):
                if n < B:
                    e.dma_start(mem.tok[:, n * TC:(n + 1) * TC], x[n]).then_inc(x_loaded[n], 16)
                e.dma_start(ada_w[:, :, n * D:(n + 1) * D], w[:, :, n * D:(n + 1) * D]).then_inc(w_loaded[n], 16)

        @block.gpsimd
        def _(e):
            e.memset(mem.ident[:, :], 0.0).then_inc(zeroed, 1)
            e.memset(mem.sel[:, :, :], 0.0).then_inc(zeroed, 1)
            e.wait_ge(zeroed, 2)
            e.affine_select(out=mem.ident[:, :], in_=mem.ident[:, :], compare_op=ALU.not_equal, fill=1.0,
                            base=0, pattern=[[-1, P]], channel_multiplier=1).then_inc(mem.const_ready, 1)
            e.affine_select(out=mem.sel[:, :, :], in_=mem.sel[:, :, :], compare_op=ALU.not_equal, fill=1.0,
                            base=0, pattern=[[-1, B], [0, P]], channel_multiplier=1).then_inc(mem.const_ready, 1)

        @block.scalar
        def _(e):
            row = "(o n) -> o n"
            e.dma_start(mem.out_b[:, :], a["out_b"].rearrange(row, o=1).broadcast_to((P, D))).then_inc(mem.vec_loaded, 16)
            e.dma_start(mem.b2[:, :], a["ffn_b2"].rearrange(row, o=1).broadcast_to((P, D))).then_inc(mem.vec_loaded, 16)
            ln_act(e)
            for k in range(2):
                for b in range(B):
                    e.wait_ge(gate_done, k * B + b + 1)
                    e.activation(mem.gate[:, k, b], bank[b % 2][:, :], ACT.Copy).then_inc(gate_ready, 1)

        @block.tensor
        def _(e):
            e.wait_ge(mem.const_ready, 2)
            e.wait_ge(cond_loaded, 16)
            for c in range(DC):
                last = e.transpose(turned_bank[:, c * B:(c + 1) * B], cond[:, c * P:(c + 1) * P], mem.ident[0:B, 0:B])
            last.then_inc(cond_turned, 1)
            e.wait_ge(rows_loaded, 80)
            e.transpose(bank[3][:, 256:256 + VECS], vec_rows, mem.ident[0:VECS, 0:VECS]).then_inc(rows_turned, 1)
            e.wait_ge(condT_ready, 1)
            for n in range(6):
                e.wait_ge(w_loaded[n], 16)
                if n >= 2:
                    e.wait_ge(ada_ready, n - 1)
                for c in range(DC):
                    last = e.matmul(bank[n % 2][0:B, :], mem.condT[:, c], ada_w[:, c, n * D:(n + 1) * D],
                                    start=(c == 0), stop=(c == DC - 1))
                last.then_inc(ada_done, 1)
            e.wait_ge(ada_ready, 6)
            for i, part in enumerate(PARTS):
                for c in range(DC):
                    at = part * D + c * P
                    last = e.transpose(bank[3][:, (i * DC + c) * B:(i * DC + c + 1) * B], ada[:, at:at + P],
                                       mem.ident[0:B, 0:B])
            last.then_inc(ada_turned, 1)
            ln_pe(e)
            for k, part in enumerate((2, 5)):
                for b in range(B):
                    if k * B + b >= 2:
                        e.wait_ge(gate_ready, k * B + b - 1)
                    e.matmul(bank[b % 2][:, :], mem.sel[:, b, :], ada[:, part * D:(part + 1) * D],
                             start=True, stop=True).then_inc(gate_done, 1)

        @block.vector
        def _(e):
            e.wait_ge(cond_turned, 1)
            e.tensor_copy(mem.condT[:, :, :].rearrange("p c b -> p (c b)"), turned_bank[:, 0:DC * B]).then_inc(condT_ready, 1)
            e.wait_ge(rows_turned, 1)
            e.tensor_copy(mem.vecT[:, :], bank[3][:, 256:256 + VECS]).then_inc(mem.vecT_ready, 1)
            e.wait_ge(adab_loaded, 16)
            for n in range(6):
                e.wait_ge(ada_done, n + 1)
                e.tensor_tensor(ada[:, n * D:(n + 1) * D], bank[n % 2][0:B, :], ada_b[:, n * D:(n + 1) * D],
                                ALU.add).then_inc(ada_ready, 1)
            e.wait_ge(ada_turned, 1)
            for i in range(4):
                part = bank[3][:, i * DC * B:(i + 1) * DC * B]
                e.tensor_scalar(mem.adaT[:, i].rearrange("p c b -> p (c b)"), part, float(i % 2), None,
                                ALU.add).then_inc(adaT_ready, 1)
            ln_dve(e, lambda e, b: e.wait_ge(x_loaded[b], 16))


def attention(nc, mem, a):
    UNITS = 2 * B
    at = [0]

    def place(*shape):
        n = 1
        for k in shape:
            n *= k
        at[0] += n
        return mem.cut(at[0] - n, list(shape))

    def parts(name, *shape):
        got = []
        for part in ("hi", "lo"):
            got.append(mem.rounded(f"{name}_{part}", mem.work, at[0], list(shape)))
            place(*shape)
        return got

    q, k = parts("q", T), parts("k", T)
    v_raw = place(T)
    v = parts("v", TC * DH)
    probs = place(TC, T)
    probsT = parts("probsT", TC, T)
    oT = parts("oT", T)
    scale = place(DC, DH)
    ones = place(DC * 3 * DH)
    assert at[0] <= 13952
    WN = DC * 3 * DH
    w_hi, w_lo = ([mem.rounded(f"w_{part}{i}", mem.work, 13952 + (2 * h + i) * WN, [WN]) for i in range(2)]
                  for h, part in enumerate(("hi", "lo")))
    ow_hi, ow_lo = ([mem.rounded(f"ow_{part}{i}", mem.work, 20096 + (2 * h + i) * D, [D]) for i in range(2)]
                    for h, part in enumerate(("hi", "lo")))
    w_raw = [mem.cut(13952 + (2 + i) * WN, [WN]) for i in range(2)]
    ow_raw = [mem.cut(20096 + (2 + i) * D, [D]) for i in range(2)]
    feat_hi = mem.rounded("feat_hi", mem.tok, 0, [DC, B, T])
    feat_lo = mem.rounded("feat_lo", mem.feat, 0, [DC, B, T])
    pair_bias = mem.small[:, 16:22].rearrange("p (t i) -> p t i", t=3)
    nmax, rinv = mem.small[:, 0:TC], mem.small[:, 4:4 + TC]
    rsum = [mem.small[:, 8 + TC * n:8 + TC * (n + 1)] for n in range(2)]

    def chunk(w, c, t):
        return w[:, :].rearrange("p (k t d) -> p k t d", k=DC, t=3)[:, c, t]

    with ExitStack() as ctx:
        def sem(name):
            return ctx.enter_context(nc.semaphore(name))

        w_loaded = [sem(f"head_loaded{i}") for i in range(2)]
        scale_set, w_scaled, w_rounded = sem("scale_set"), sem("w_scaled"), sem("w_rounded")
        w_split = [sem(f"head_split{i}") for i in range(2)]
        feat_rounded, x_reloaded = sem("feat_rounded"), mem.x_reloaded
        feat_split = [sem(f"feat_split{b}") for b in range(B)]
        acc_done, bias_scaled, bias_ready = sem("acc_done"), sem("bias_scaled"), sem("bias_ready")
        qkv_done, qk_hi, qkv_ready = sem("qkv_done"), sem("qk_hi"), sem("qkv_ready")
        score_done, max_ready, exp_ready, inv_ready = (
            sem(n) for n in ("score_done", "max_ready", "exp_ready", "inv_ready"))
        v_turned, v_hi, v_ready, p_turned, pT_hi, pT_ready = (
            sem(n) for n in ("v_turned", "v_hi", "v_ready", "p_turned", "pT_hi", "pT_ready"))
        o_done, oT_hi, oT_ready, proj_done = sem("o_done"), sem("oT_hi"), sem("oT_ready"), sem("proj_done")
        bank_qkv, bank_s, bank_o = mem.psum[0:2], mem.psum[2:4], mem.psum[6:8]
        turned_bank = [mem.psum[5], mem.psum[4]] + bank_s
        block = ctx.enter_context(nc.Block())
        PAIRS = HEADS // 2

        @block.sync
        def _(e):
            wq = a["qkv_w"].rearrange("(k p) (t h d) -> h p k t d", p=P, t=3, h=HEADS)
            wo = a["out_w"].rearrange("(h d) n -> h d n", h=HEADS)

            def load(i, head):
                into = w_raw[i].rearrange("p (k t d) -> p k t d", k=DC, t=3)
                for t in range(3):
                    e.dma_start(into[:, :, t], wq[head][:, :, t]).then_inc(w_loaded[i], 16)
                e.dma_start(ow_raw[i], wo[head]).then_inc(w_loaded[i], 16)

            for i in range(2):
                load(i, i)
            with e.Fori(0, PAIRS - 1) as g:
                for i in range(2):
                    e.wait_ge(acc_done, (UNITS * g + B * (i + 1)) * TC)
                    load(i, 2 * g + 2 + i)
            e.wait_ge(qkv_done, 3 * UNITS * PAIRS)
            x = a["x"].rearrange("b (t p) d -> b p t d", p=P)
            for b in range(B):
                e.dma_start(mem.tok[:, b * TC:(b + 1) * TC], x[b]).then_inc(x_reloaded[b], 16)
            w1 = mem.cut(13952, [DC, MLP])
            from_w1 = a["ffn_w1"].rearrange("(c p) n -> p c n", p=P)
            e.dma_start(w1[:, 0:DC - 1], from_w1[:, 0:DC - 1]).then_inc(mem.w1_loaded, 16)
            e.wait_ge(proj_done, TC * UNITS * PAIRS)
            e.dma_start(w1[:, DC - 1], from_w1[:, DC - 1]).then_inc(mem.w1_loaded, 16)

        @block.gpsimd
        def _(e):
            def split(i, count, g):
                e.wait_ge(w_loaded[i], 64 * (g + 1))
                wq = w_raw[i].rearrange("p (k t d) -> p k t d", k=DC, t=3)[:, :, 0]
                e.tensor_tensor(wq, wq, scale, ALU.mult).then_inc(w_scaled, 1)
                e.wait_ge(w_scaled, count + 1)
                e.tensor_tensor(w_hi[i][:, :], w_raw[i], ones, ALU.mult).then_inc(w_rounded, 1)
                e.tensor_tensor(ow_hi[i][:, :], ow_raw[i], ones[:, 0:D], ALU.mult).then_inc(w_rounded, 1)
                e.wait_ge(w_rounded, 2 * count + 2)
                e.tensor_tensor(w_lo[i][:, :], w_raw[i], w_hi[i][:, :], ALU.subtract).then_inc(w_split[i], 1)
                e.tensor_tensor(ow_lo[i][:, :], ow_raw[i], ow_hi[i][:, :], ALU.subtract).then_inc(w_split[i], 1)

            e.memset(scale, QSCALE).then_inc(scale_set, 1)
            e.memset(ones, 1.0).then_inc(scale_set, 1)
            e.wait_ge(scale_set, 2)
            split(0, 0, 0)
            for b in (2, 3):
                e.wait_ge(feat_rounded, b + 1)
                e.tensor_tensor(feat_lo[:, :, b], mem.feat[:, :, b], feat_hi[:, :, b], ALU.subtract).then_inc(feat_split[b], 1)
            split(1, 1, 0)
            with e.Fori(1, PAIRS) as g:
                for i in range(2):
                    split(i, 2 * g + i, g)

        def pe_three(e, out, x, y, start, stop):
            e.matmul(out, x[0], y[0], start=start, stop=False)
            e.matmul(out, x[0], y[1], start=False, stop=False)
            return e.matmul(out, x[1], y[0], start=False, stop=stop)

        def pe_qkv(e, g, u, first):
            i, b, n, pair = (u // B) % 2, u % B, 3 * u, g + u // UNITS
            if b == 0:
                e.wait_ge(w_split[i], 2 * (pair + 1))
            if first and u < B:
                e.wait_ge(feat_split[b], 1)
            for t in range(3):
                m = n + t
                if not (first and m < 2):
                    e.wait_ge(qkv_ready, 3 * UNITS * g + m - 1)
                for c in range(DC):
                    last = pe_three(e, bank_qkv[m % 2][:, :], (chunk(w_hi[i], c, t), chunk(w_lo[i], c, t)),
                                    (feat_hi[:, c, b], feat_lo[:, c, b]), c == 0, c == DC - 1)
                last.then_inc(qkv_done, 1)

        def pe_project(e, g, u, t, first):
            i, U, m = (u // B) % 2, UNITS * g + u, 5 * u + 1 + t
            if t == 0:
                e.wait_ge(oT_ready, U + 1)
                if not first:
                    e.wait_ge(acc_done, TC * U)
            elif t >= 2:
                e.wait_ge(acc_done, TC * U + t - 1)
            tile = slice(t * P, (t + 1) * P)
            pe_three(e, bank_o[m % 2][:, :], (oT[0][:, tile], oT[1][:, tile]), (ow_hi[i][:, :], ow_lo[i][:, :]),
                     True, True).then_inc(proj_done, 1)

        def pe_pair(e, g, first=False, final=False):
            for u in range(UNITS):
                start = first and u == 0
                U = UNITS * g + u
                if start:
                    pe_qkv(e, g, 0, first)
                e.wait_ge(qkv_ready, 3 * U + 2)
                for t in range(TC):
                    if not (start and t < 2):
                        e.wait_ge(exp_ready, TC * U + t - 1)
                    tile = slice(t * P, (t + 1) * P)
                    pe_three(e, bank_s[t % 2][:, :], (q[0][:, tile], q[1][:, tile]), (k[0][:, :], k[1][:, :]), True, True).then_inc(score_done, 1)
                    if t == 1:
                        e.wait_ge(qkv_ready, 3 * U + 3)
                        if not start:
                            e.wait_ge(pT_ready, TC * U)
                        for s in range(TC):
                            last = e.transpose(turned_bank[1][:, s * P:(s + 1) * P], v_raw[:, s * P:(s + 1) * P], mem.ident[:, :])
                        last.then_inc(v_turned, 1)
                    if t % 2 == 1 and not start:
                        for n in (t - 1, t):
                            pe_project(e, g, u - 1, n, first and u == 1)
                if not (final and u == UNITS - 1):
                    pe_qkv(e, g, u + 1, first)
                e.wait_ge(exp_ready, TC * U + TC)
                for s in range(TC):
                    if s == 1:
                        e.wait_ge(v_ready, U + 1)
                    for t in range(TC):
                        last = e.transpose(turned_bank[s][:, t * P:(t + 1) * P], probs[:, t, s * P:(s + 1) * P],
                                           mem.ident[:, :])
                    last.then_inc(p_turned, 1)
                if not start:
                    e.wait_ge(acc_done, TC * U - 1)
                for s in range(TC):
                    e.wait_ge(pT_ready, TC * U + s + 1)
                    keys = slice(s * DH, (s + 1) * DH)
                    last = pe_three(e, bank_o[(5 * u) % 2][:, :], (v[0][:, keys], v[1][:, keys]),
                                    (probsT[0][:, s], probsT[1][:, s]), s == 0, s == TC - 1)
                last.then_inc(o_done, 1)
            if final:
                for t in range(TC):
                    pe_project(e, g, UNITS - 1, t, False)

        @block.tensor
        def _(e):
            pe_pair(e, 0, first=True)
            with e.Fori(1, PAIRS - 1) as g:
                pe_pair(e, g)
            pe_pair(e, PAIRS - 1, final=True)

        def act_qkv(e, g, u):
            i, U = (u // B) % 2, UNITS * g + u
            if u % B == 0:
                e.wait_ge(bias_ready, 2 * g + u // B + 1)
            for t in range(2):
                e.wait_ge(qkv_done, 3 * U + t + 1)
                e.activation((q, k)[t][0][:, :], bank_qkv[(3 * u + t) % 2][:, :], ACT.Identity,
                             bias=pair_bias[:, t, i:i + 1]).then_inc(qk_hi, 1)
            e.wait_ge(qkv_done, 3 * U + 3)
            e.wait_ge(qkv_ready, 3 * U + 2)
            e.activation(v_raw, bank_qkv[(3 * u + 2) % 2][:, :], ACT.Identity,
                         bias=pair_bias[:, 2, i:i + 1]).then_inc(qkv_ready, 1)

        def act_pair(e, g, first=False, final=False):
            for u in range(UNITS):
                U = UNITS * g + u
                start = first and u == 0
                if start:
                    act_qkv(e, g, 0)
                for t in range(TC):
                    e.wait_ge(max_ready, TC * U + t + 1)
                    if t == 0 and not start:
                        e.wait_ge(p_turned, TC * U)
                        if not (first and u == 1):
                            e.wait_ge(inv_ready, U - 1)
                    e.activation(probs[:, t], bank_s[t % 2][:, :], ACT.Exp, bias=nmax[:, t:t + 1],
                                 accum_out=rsum[u % 2][:, t:t + 1]).then_inc(exp_ready, 1)
                e.wait_ge(v_turned, U + 1)
                if not start:
                    e.wait_ge(o_done, U)
                e.activation(v[0][:, :], turned_bank[1][:, :], ACT.Copy).then_inc(v_hi, 1)
                if not (final and u == UNITS - 1):
                    act_qkv(e, g, u + 1)
                for s in range(TC):
                    e.wait_ge(p_turned, TC * U + s + 1)
                    e.activation(probsT[0][:, s], turned_bank[s][:, :], ACT.Copy).then_inc(pT_hi, 1)
                e.wait_ge(o_done, U + 1)
                if not start:
                    e.wait_ge(proj_done, TC * U)
                e.activation(oT[0][:, :], bank_o[(5 * u) % 2][:, :], ACT.Copy).then_inc(oT_hi, 1)

        @block.scalar
        def _(e):
            e.preload_act_table(ACT.Exp)
            for b in range(B):
                e.activation(feat_hi[:, :, b], mem.feat[:, :, b], ACT.Copy).then_inc(feat_rounded, 1)
            act_pair(e, 0, first=True)
            with e.Fori(1, PAIRS - 1) as g:
                act_pair(e, g)
            act_pair(e, PAIRS - 1, final=True)

        def dve_rest(e, out, bank, hi):
            return e.tensor_tensor(out, bank[:, :], hi, ALU.subtract)

        def dve_qk(e, g, u):
            i, U = (u // B) % 2, UNITS * g + u
            for t in range(2):
                e.wait_ge(qk_hi, 2 * U + t + 1)
                hi, lo = (q, k)[t]
                e.scalar_tensor_tensor(out=lo[:, :], in0=bank_qkv[(3 * u + t) % 2][:, :], scalar=pair_bias[:, t, i:i + 1],
                                       in1=hi[:, :], op0=ALU.add, op1=ALU.subtract).then_inc(qkv_ready, 1)
                if t == 0:
                    e.wait_ge(qkv_ready, 3 * U + 1)

        def dve_bias(e, i, head):
            e.tensor_scalar(pair_bias[:, :, i:i + 1], mem.qkv_bT[:, :, bass.ds(head, 1)], 0.0, None, ALU.add).then_inc(bias_ready, 1)

        def dve_project(e, g, u, tiles, first):
            b, U = u % B, UNITS * g + u
            for t in tiles:
                e.wait_ge(proj_done, TC * U + t + 1)
                tile = mem.acc[:, b * TC + t]
                e.scalar_tensor_tensor(out=tile, in0=bank_o[(5 * u + 1 + t) % 2][:, :], scalar=rinv[:, t:t + 1],
                                       in1=mem.out_b[:, :] if first and u < B else tile,
                                       op0=ALU.mult, op1=ALU.add).then_inc(acc_done, 1)

        def dve_pair(e, g, first=False, final=False):
            for u in range(UNITS):
                U = UNITS * g + u
                start = first and u == 0
                if start:
                    dve_qk(e, g, 0)
                for t in range(TC):
                    e.wait_ge(score_done, TC * U + t + 1)
                    if t == 0 and not start:
                        e.wait_ge(exp_ready, TC * U)
                    e.tensor_reduce(nmax[:, t:t + 1], bank_s[t % 2][:, :], AX.X, ALU.max, negate=True).then_inc(max_ready, 1)
                    if t % 2 == 1 and not start:
                        dve_project(e, g, u - 1, (t - 1, t), first)
                e.wait_ge(exp_ready, TC * U + TC)
                if not start:
                    e.wait_ge(acc_done, TC * U)
                e.reciprocal(rinv, rsum[u % 2]).then_inc(inv_ready, 1)
                e.wait_ge(inv_ready, U + 1)
                if u == 0:
                    if not first:
                        e.wait_ge(qkv_ready, 3 * U)
                        dve_bias(e, 1, 2 * g + 1)
                elif u == B and not final:
                    e.wait_ge(qkv_ready, 3 * U)
                    dve_bias(e, 0, 2 * g + 2)
                e.wait_ge(v_hi, U + 1)
                dve_rest(e, v[1][:, :], turned_bank[1], v[0][:, :]).then_inc(v_ready, 1)
                if not (final and u == UNITS - 1):
                    dve_qk(e, g, u + 1)
                for s in range(TC):
                    e.wait_ge(pT_hi, TC * U + s + 1)
                    dve_rest(e, probsT[1][:, s], turned_bank[s], probsT[0][:, s]).then_inc(pT_ready, 1)
                e.wait_ge(oT_hi, U + 1)
                dve_rest(e, oT[1][:, :], bank_o[(5 * u) % 2], oT[0][:, :]).then_inc(oT_ready, 1)
            if final:
                dve_project(e, g, UNITS - 1, range(TC), first)

        @block.vector
        def _(e):
            for b in (0, 1):
                e.wait_ge(feat_rounded, b + 1)
                e.tensor_tensor(feat_lo[:, :, b], mem.feat[:, :, b], feat_hi[:, :, b], ALU.subtract).then_inc(feat_split[b], 1)
            e.tensor_scalar(mem.qkv_bT[:, 0], mem.qkv_bT[:, 0], QSCALE, None, ALU.mult).then_inc(bias_scaled, 1)
            e.wait_ge(bias_scaled, 1)
            for i in range(2):
                dve_bias(e, i, i)
            e.wait_ge(bias_ready, 2)
            e.wait_ge(mem.vec_loaded, 32)
            dve_pair(e, 0, first=True)
            with e.Fori(1, PAIRS - 1) as g:
                dve_pair(e, g)
            dve_pair(e, PAIRS - 1, final=True)


def feed_forward(nc, mem, a):
    w1 = mem.cut(13952, [DC, MLP])
    w2 = mem.cut(0, [MC, D])
    feat_hi = mem.rounded("x2_hi", mem.acc, 0, [DC, B, T])
    feat_lo = mem.rounded("x2_lo", mem.feat, 0, [DC, B, T])
    w1_hi, w1_lo, w2_hi, w2_lo = (
        [mem.rounded(f"{name}{n}", mem.work, 8192 + (2 * k + n) * D, [D]) for n in range(2)]
        for k, name in enumerate(("w1_hi", "w1_lo", "w2_hi", "w2_lo")))
    hT_hi = [mem.rounded(f"hT_hi{n}", mem.work, 12288 + n * T, [T]) for n in range(2)]
    hT = [mem.cut(13312, [T]), mem.out_b[:, :]]
    hT_lo = [mem.rounded("hT_lo0", mem.work, 13312, [T]), mem.rounded("hT_lo1", mem.out_b, 0, [T])]
    norm = mem.work[:, 9216:9216 + 2 * TC * D].rearrange("p (r t d) -> p r t d", r=2, t=TC)
    ffn = [mem.gate[:, 0, t] for t in range(TC)]
    with ExitStack() as ctx:
        def sem(name):
            return ctx.enter_context(nc.semaphore(name))

        w2_loaded, gated, resid = sem("w2_loaded"), sem("gated"), sem("resid")
        h_done, hT_ready, y_done, y_out, gated_ffn, x_added = (
            sem(n) for n in ("h_done", "hT_ready", "y_done", "y_out", "gated_ffn", "x_added"))
        ffn_added, h_ready, h_hi = (sem(n) for n in ("ffn_added", "h_ready", "h_hi"))
        w1_rounded, w1_split, w2_rounded, w2_split = (
            sem(n) for n in ("w1_rounded", "w1_split", "w2_rounded", "w2_split"))
        feat_rounded, feat_split, feat_split_pool = (
            sem(n) for n in ("x2_rounded", "x2_split", "x2_split_pool"))
        ln_dve, ln_act, ln_pe, turned, act_out, dve_out = layernorm_engines(nc, ctx, mem, "ln2", mem.acc, 2, norm, lambda e: None)
        bank_h, bank_y = mem.psum[0:2], mem.psum[4:8]
        block = ctx.enter_context(nc.Block())

        def chunked(w):
            return w[:, :].rearrange("p (c n) -> p c n", c=DC)

        @block.sync
        def _(e):
            e.dma_start(w2, a["ffn_w2"].rearrange("(c p) n -> p c n", p=P)).then_inc(w2_loaded, 16)

        @block.gpsimd
        def _(e):
            for t in range(NTILE):
                e.wait_ge(resid, t + 1)
                e.tensor_tensor(mem.tok[:, t], mem.tok[:, t], mem.acc[:, t], ALU.add).then_inc(x_added, 1)

            def rest_of_w1(m, n):
                e.wait_ge(w1_rounded, n + 1)
                e.tensor_tensor(chunked(w1_lo[m % 2]), w1[:, :, m * P:(m + 1) * P], chunked(w1_hi[m % 2]),
                                ALU.subtract).then_inc(w1_split, 1)

            def rest_of_w2(m, n):
                e.wait_ge(w2_rounded, n + 1)
                e.tensor_tensor(w2_lo[m % 2][:, :], w2[:, m], w2_hi[m % 2][:, :], ALU.subtract).then_inc(w2_split, 1)

            def batch(b):
                for m in range(MC):
                    n = MC * b + m
                    rest_of_w1((m + 2) % MC, n + 2)
                    rest_of_w2((m + 1) % MC, n + 1)
                    if isinstance(b, int) and m in (1, 3):
                        other = 2 + m // 2
                        e.wait_ge(feat_rounded, other + 1)
                        e.tensor_tensor(feat_lo[:, :, other], mem.feat[:, :, other], feat_hi[:, :, other],
                                        ALU.subtract).then_inc(feat_split_pool, 1)

            rest_of_w1(0, 0)
            rest_of_w1(1, 1)
            rest_of_w2(0, 0)
            batch(0)
            with e.Fori(1, B) as b:
                batch(b)

        @block.tensor
        def _(e):
            ln_pe(e)
            e.wait_ge(feat_split, 1)

            def three(out, x_hi, x_lo, y_hi, y_lo, start, stop):
                e.matmul(out, x_hi, y_hi, start=start, stop=False)
                e.matmul(out, x_hi, y_lo, start=False, stop=False)
                return e.matmul(out, x_lo, y_hi, start=False, stop=stop)

            def batch(b):
                def hidden(m):
                    n = MC * b + m
                    e.wait_ge(w1_split, n + 1)
                    if not (isinstance(b, int) and m < 2):
                        e.wait_ge(h_ready, n - 1)
                    for c in range(DC):
                        hi, lo = (f[:, c, bass.ds(b, 1)].rearrange("p o t -> p (o t)") for f in (feat_hi, feat_lo))
                        last = three(bank_h[m % 2][:, :], chunked(w1_hi[m % 2])[:, c], chunked(w1_lo[m % 2])[:, c],
                                     hi, lo, c == 0, c == DC - 1)
                    last.then_inc(h_done, 1)

                hidden(0)
                for m in range(MC):
                    if m + 1 < MC:
                        hidden(m + 1)
                    e.wait_ge(hT_ready, MC * b + m + 1)
                    e.wait_ge(w2_split, MC * b + m + 1)
                    for t in range(TC):
                        if m == 0 and t == 0 and not isinstance(b, int):
                            e.wait_ge(y_out, TC * b)
                        tile = slice(t * P, (t + 1) * P)
                        last = three(bank_y[t][:, :], hT_hi[m % 2][:, tile], hT_lo[m % 2][:, tile],
                                     w2_hi[m % 2][:, :], w2_lo[m % 2][:, :], m == 0, m == MC - 1)
                    last.then_inc(y_done, 1)
                if isinstance(b, int):
                    e.wait_ge(feat_split, 2)
                    e.wait_ge(feat_split_pool, 2)

            batch(0)
            with e.Fori(1, B) as b:
                batch(b)

        @block.scalar
        def _(e):
            ln_act(e)
            e.preload_act_table(ACT.Gelu)
            e.wait_ge(turned, DC * B)
            e.wait_ge(x_added, NTILE)
            e.wait_ge(act_out, 2 * B)
            e.wait_ge(dve_out, 2 * B)

            def round_feat(b):
                e.activation(feat_hi[:, :, b], mem.feat[:, :, b], ACT.Copy).then_inc(feat_rounded, 1)

            def round_w1(m):
                e.activation(chunked(w1_hi[m % 2]), w1[:, :, m * P:(m + 1) * P], ACT.Copy).then_inc(w1_rounded, 1)

            def round_w2(m):
                e.activation(w2_hi[m % 2][:, :], w2[:, m], ACT.Copy).then_inc(w2_rounded, 1)

            def batch(b):
                for m in range(MC):
                    n = MC * b + m
                    e.wait_ge(h_done, n + 1)
                    e.activation(hT[m % 2], bank_h[m % 2][:, :], ACT.Gelu, bias=mem.b1T[:, m:m + 1]).then_inc(h_ready, 1)
                    round_w1((m + 2) % MC)
                    if not (isinstance(b, int) and m == 0):
                        e.wait_ge(y_done, n)
                    round_w2((m + 1) % MC)

            round_feat(0)
            e.wait_ge(mem.w1_loaded, 32)
            e.wait_ge(w2_loaded, 16)
            round_w1(0)
            round_w1(1)
            round_w2(0)
            for b in range(1, B):
                round_feat(b)
            batch(0)
            with e.Fori(1, B) as b:
                batch(b)

        @block.vector
        def _(e):
            def gate_residual(e, b):
                for t in range(b * TC, (b + 1) * TC):
                    e.tensor_tensor(mem.acc[:, t], mem.acc[:, t], mem.gate[:, 0, b], ALU.mult).then_inc(gated, 1)
                e.wait_ge(mem.x_reloaded[b], 16)
                for t in range(b * TC, (b + 1) * TC):
                    e.wait_ge(gated, t + 1)
                    e.tensor_tensor(mem.acc[:, t], mem.acc[:, t], mem.tok[:, t], ALU.add).then_inc(resid, 1)
                e.wait_ge(resid, (b + 1) * TC)

            ln_dve(e, gate_residual)
            for b in range(2):
                e.wait_ge(feat_rounded, b + 1)
                e.tensor_tensor(feat_lo[:, :, b], mem.feat[:, :, b], feat_hi[:, :, b], ALU.subtract).then_inc(feat_split, 1)

            def add_ffn(b):
                gate = mem.gate[:, 1, bass.ds(b, 1)].rearrange("p o d -> p (o d)")
                for t in range(TC):
                    e.wait_ge(y_out, TC * b + t + 1)
                    e.tensor_tensor(ffn[t], ffn[t], gate, ALU.mult).then_inc(gated_ffn, 1)
                for t in range(TC):
                    e.wait_ge(gated_ffn, TC * b + t + 1)
                    tile = mem.tok[:, bass.ds(TC * b + t, 1)].rearrange("p o d -> p (o d)")
                    e.tensor_tensor(tile, tile, ffn[t], ALU.add).then_inc(ffn_added, 1)

            def batch(b):
                for m in range(MC):
                    n = MC * b + m
                    e.wait_ge(h_ready, n + 1)
                    e.tensor_copy(hT_hi[m % 2][:, :], hT[m % 2]).then_inc(h_hi, 1)
                    e.wait_ge(h_hi, n + 1)
                    e.tensor_tensor(hT_lo[m % 2][:, :], hT[m % 2], hT_hi[m % 2][:, :], ALU.subtract).then_inc(hT_ready, 1)
                    if m == 2 and not isinstance(b, int):
                        add_ffn(b - 1)
                e.wait_ge(y_done, MC * b + MC)
                if not isinstance(b, int):
                    e.wait_ge(ffn_added, TC * b)
                for t in range(TC):
                    e.tensor_tensor(ffn[t], bank_y[t][:, :], mem.b2[:, :], ALU.add).then_inc(y_out, 1)

            batch(0)
            with e.Fori(1, B) as b:
                batch(b)
            add_ffn(B - 1)


def convolution(nc, mem, a):
    coupling = mem.cut(0, [DC, D])
    couplingT = mem.cut(2048, [DC, D])
    with ExitStack() as ctx:
        def sem(name):
            return ctx.enter_context(nc.semaphore(name))

        turned, copied, tap, tap1 = sem("x_turned"), sem("x_copied"), sem("tap"), sem("tap_first")
        c_turned = sem("coupling_turned")
        bank = mem.psum[0:4]
        block = ctx.enter_context(nc.Block())

        @block.sync
        def _(e):
            e.dma_start(coupling, a["coupling"].rearrange("(c p) n -> p c n", p=P)).then_inc(mem.coupling_loaded, 16)

        @block.tensor
        def _(e):
            n = 0
            for b in range(B):
                for c in range(DC):
                    if n >= 4:
                        e.wait_ge(tap, n - 3)
                    for t in range(TC):
                        last = e.transpose(bank[n % 4][:, t * P:(t + 1) * P], mem.tok[:, b * TC + t, c * P:(c + 1) * P],
                                           mem.ident[:, :])
                    last.then_inc(turned, 1)
                    n += 1
            e.wait_ge(mem.coupling_loaded, 16)
            for c in range(DC):
                for r in range(DC):
                    last = e.transpose(mem.psum[4 + c][:, r * P:(r + 1) * P], coupling[:, r, c * P:(c + 1) * P],
                                       mem.ident[:, :])
                last.then_inc(c_turned, 1)

        @block.scalar
        def _(e):
            for n in range(B * DC):
                b, c = n // DC, n % DC
                e.wait_ge(turned, n + 1)
                e.activation(mem.feat[:, c, b], bank[n % 4][:, :], ACT.Identity,
                             bias=mem.convbT[:, c:c + 1]).then_inc(copied, 1)
            for c in range(DC):
                e.wait_ge(c_turned, c + 1)
                e.activation(couplingT[:, c], mem.psum[4 + c][:, :], ACT.Copy).then_inc(copied, 1)

        @block.vector
        def _(e):
            for n in range(B * DC):
                b, c = n // DC, n % DC
                x = bank[n % 4]
                e.wait_ge(copied, n + 1)
                for back in range(B):
                    if back:
                        e.wait_ge(tap1, n * (B - 1) + back)
                    out = mem.feat[:, c, b, back:]
                    e.scalar_tensor_tensor(out=out, in0=x[:, 0:T - back], scalar=mem.condT[:, c, B - 1 - back:B - back],
                                           in1=out, op0=ALU.mult, op1=ALU.add).then_inc(tap if back == B - 1 else tap1, 1)



def coupled_scan(nc, mem, a):
    N = DC * B
    QT = P // 4
    couplingT = mem.cut(2048, [DC, D])
    at = [4096]

    def state(n=N):
        at[0] += n
        return mem.cut(at[0] - n, [n])

    q, q2, q3, q4, q_new = (state() for _ in range(5))
    p, p2, p3, p4, p_new = (state() for _ in range(5))
    v = [state() for _ in range(4)]
    dq = [state() for _ in range(3)]
    square, cubic, drive, bias, dq_sum, v_mid, v_ends, v_sum, lessp0, lessp, lead_dq = (
        state() for _ in range(11))
    lead, base, partial = ([state() for _ in range(2)] for _ in range(3))
    tanh_q = [state() for _ in range(2)]
    back = [state(P // 2) for _ in range(2)]
    HALF = [slice(h * N // 2, (h + 1) * N // 2) for h in range(2)]
    idle = mem.cut(at[0], [P]).bitcast(BF16)[:, 0:P]
    x = mem.feat[:, :, :, :].rearrange("p c b t -> p (c b) t")
    C = [H_STEP / 2, H_STEP / 2, H_STEP, H_STEP / 6]
    Q, PP = [q, q2, q3, q4], [p, p2, p3, p4]
    with ExitStack() as ctx:
        def sem(name):
            return ctx.enter_context(nc.semaphore(name))

        set_up, vec, q_ready, q_clipped, v_ready, p_ready, lessp_ready = (
            sem(n) for n in ("scan_set_up", "vec", "q_ready", "q_clipped", "v_ready", "p_ready", "lessp_ready"))
        tanh_ready, m_ready, dq_ready, v_sums_ready = (
            sem(n) for n in ("tanh_ready", "m_ready", "dq_ready", "v_sums_ready"))
        STEPS = 10
        assert (T - 2) % STEPS == 0
        bank = [mem.psum[0:2], mem.psum[2:4]]
        block = ctx.enter_context(nc.Block())

        @block.scalar
        def _(e):
            e.preload_act_table(ACT.Tanh)
            with e.Fori(0, T) as t:
                for i in range(4):
                    for h in range(2):
                        e.wait_ge(q_ready, 8 * t + 2 * i + h + 1)
                        e.activation(tanh_q[i % 2][:, HALF[h]], (Q[i] if i else q_new)[:, HALF[h]],
                                     ACT.Tanh).then_inc(tanh_ready, 1)

        @block.tensor
        def _(e):
            e.wait_ge(set_up, 6 + B)

            def share(i, half, chunks):
                for c in chunks:
                    for j in range(4):
                        cols = couplingT[:, c].rearrange("p (s j k) -> p j s k", s=DC, j=4)[:, j, 2 * half:2 * half + 2]
                        last = e.matmul(bank[i % 2][half][QT * j:QT * j + B, 0:P // 2],
                                        tanh_q[i % 2][:, B * c:B * c + B], cols,
                                        start=(c == 0), stop=(c == DC - 1), tile_position=(0, QT * j))
                return last

            with e.Fori(0, T) as t:
                for i in range(4):
                    e.wait_ge(tanh_ready, 8 * t + 2 * i + 1)
                    share(i, 0, (0, 1))
                    share(i, 1, (0,))
                    e.wait_ge(tanh_ready, 8 * t + 2 * i + 2)
                    share(i, 0, (2, 3)).then_inc(m_ready, 1)
                    share(i, 1, (1, 2, 3)).then_inc(m_ready, 1)
                    for _ in range(KEEP_WARM):
                        e.matmul(mem.psum[4][:, 0:P], idle, idle, start=True, stop=True)

        @block.gpsimd
        def _(e):
            e.wait_ge(set_up, 7 + B)
            with e.Fori(0, T) as t:
                for i in range(4):
                    if i > 0:
                        e.wait_ge(q_ready, 8 * t + 2 * i + 2)
                        if i == 1:
                            e.wait_ge(q_clipped, t + 1)
                        e.tensor_tensor(dq[i - 1], Q[i], q, ALU.subtract).then_inc(dq_ready, 1)
                    if i < 3:
                        e.wait_ge(p_ready, 3 * t + i + 1)
                        e.tensor_tensor(lessp, drive, PP[i + 1], ALU.subtract).then_inc(lessp_ready, 1)
                    if i == 2:
                        e.wait_ge(v_ready, 4 * t + 3)
                        e.tensor_tensor(v_mid, v[1], v[2], ALU.add).then_inc(v_sums_ready, 1)
                    if i == 3:
                        e.wait_ge(v_ready, 4 * t + 4)
                        e.tensor_tensor(v_ends, v[0], v[3], ALU.add).then_inc(v_sums_ready, 1)

        @block.vector
        def _(e):
            for n in range(4):
                e.memset(mem.psum[n][:, 0:P // 2], 0.0).then_inc(set_up, 1)
            e.memset(idle, 0.0).then_inc(set_up, 1)
            cond = mem.condT[:, :, :].rearrange("p c b -> p (c b)")
            e.tensor_scalar(p, cond, -P_SHIFT, None, ALU.add).then_inc(set_up, 1)
            for b in range(B):
                e.tensor_scalar(bias.rearrange("p (c b) -> p c b", b=B)[:, :, b], mem.cbiasT, -P_SHIFT, None,
                                ALU.add).then_inc(set_up, 1)
            e.wait_ge(set_up, 6 + B)
            e.tensor_copy(q_new, cond).then_inc(q_ready, 2)
            e.tensor_tensor(drive, x[:, :, 0], bias, ALU.add).then_inc(set_up, 1)
            e.tensor_copy(q, cond).then_inc(q_clipped, 1)
            e.wait_ge(set_up, 7 + B)
            e.wait_ge(q_clipped, 1)
            OPS = 37

            def fma(out, in0, scalar, in1, op1=ALU.add):
                return e.scalar_tensor_tensor(out=out, in0=in0, scalar=scalar, in1=in1, op0=ALU.mult, op1=op1)

            def x_at(t):
                return x[:, :, bass.ds(t, 1)].rearrange("p n o -> p (n o)")

            def step(t, first=False, last=False):
                before = 0 if first else OPS * t - 1
                done = {}
                count = [0]

                def signal(name, instruction):
                    count[0] += 1
                    done[name] = count[0]
                    instruction.then_inc(vec, 1)

                def need(*names):
                    e.wait_ge(vec, before + max(done[n] for n in names))

                def half(i, h, beside):
                    e.wait_ge(m_ready, 8 * t + 2 * i + h + 1)
                    signal("back", e.transpose(back[h], bank[i % 2][h][:, 0:P // 2]))
                    back_at = done["back"]
                    beside()
                    done["back"] = back_at
                    need("back", "base")
                    coupled = back[h].rearrange("p (c r) -> p c r", c=DC // 2)[:, :, 0:B]
                    to = Q[i + 1] if i < 3 else q_new
                    fma(to[:, HALF[h]].rearrange("p (c b) -> p c b", b=B), coupled, C[i],
                        base[i % 2][:, HALF[h]].rearrange("p (c b) -> p c b", b=B)).then_inc(q_ready, 1)

                def nothing():
                    pass

                for i in range(4):
                    qi, pi, c, even = Q[i], PP[i], C[i], i % 2

                    def p_stage():
                        e.wait_ge(v_ready, 4 * t + i + 1)
                        fma(PP[i + 1], v[i], c * EPSILON, p).then_inc(p_ready, 1)

                    def next_lead():
                        e.wait_ge(lessp_ready, 3 * t + i + 1)
                        signal(f"lead{i + 1}", fma(lead[1 - even], lessp, C[i + 1], q))

                    if i == 0:
                        if not first:
                            e.wait_ge(q_ready, 8 * t + 2)
                            e.tensor_scalar(q, q_new, CLAMP, -CLAMP, ALU.min, ALU.max).then_inc(q_clipped, 1)
                        signal("lessp0", e.tensor_tensor(lessp0, drive, p, ALU.subtract))
                        e.wait_ge(q_clipped, t + 1)
                    if i == 3:
                        signal("partial3", fma(partial[0], qi, c, lead_dq))
                    signal("square", e.tensor_tensor(square, qi, qi, ALU.mult))
                    if i == 0:
                        signal("lead0", fma(lead[0], q, c, q))
                    elif i < 3:
                        signal("partial", fma(partial[even], qi, c, lead[even]))
                    if i > 0:
                        fma(v[i], pi, -BETA, qi).then_inc(v_ready, 1)
                    need("square")
                    signal("cubic", fma(cubic, square, -1 / 3, qi, ALU.mult))
                    if i == 0:
                        need("lead0")
                        signal("partial", fma(partial[0], lessp0, c, lead[0]))
                        fma(v[0], p, -BETA, q).then_inc(v_ready, 1)
                    elif i < 3:
                        p_stage()
                    if i < 3:
                        need("partial", "cubic")
                        signal("base", fma(base[even], cubic, c, partial[even]))
                        half(i, 0, p_stage if i == 0 else next_lead)
                        if i == 1 and not first:
                            signal("trace", e.tensor_tensor(x_at(t - 1), x_at(t - 1), q, ALU.add))
                        if i == 2:
                            e.wait_ge(dq_ready, 3 * t + 2)
                            signal("dq_sum", fma(dq_sum, dq[1], 2.0, dq[0]))

                        def lead_with_dq():
                            need("dq_sum", "lead3")
                            signal("lead_dq", fma(lead_dq, dq_sum, 1 / 3, lead[1]))

                        half(i, 1, (next_lead, nothing, lead_with_dq)[i])
                    else:
                        e.wait_ge(dq_ready, 3 * t + 3)
                        signal("partial", fma(partial[1], dq[2], 1 / 3, partial[0]))
                        if not last:
                            signal("drive", e.tensor_tensor(drive, x_at(t + 1), bias, ALU.add))
                        need("partial")
                        signal("base", fma(base[1], cubic, c, partial[1]))

                        def sum_v():
                            e.wait_ge(v_sums_ready, 2 * t + 2)
                            signal("v_sum", fma(v_sum, v_mid, 2.0, v_ends))

                        half(3, 0, sum_v)
                        need("v_sum")
                        signal("p_new", fma(p_new, v_sum, C[3] * EPSILON, p))

                        def clip_p():
                            need("p_new")
                            signal("p", e.tensor_scalar(p, p_new, CLAMP - P_SHIFT, -CLAMP - P_SHIFT, ALU.min, ALU.max))

                        half(3, 1, clip_p)
                    if i < 3:
                        e.wait_ge(q_ready, 8 * t + 2 * i + 4)
                assert last or count[0] == OPS - first, count

            step(0, first=True)
            with e.Fori(0, (T - 2) // STEPS) as k:
                for n in range(STEPS):
                    step(k * STEPS + (1 + n))
            step(T - 1, last=True)
            e.wait_ge(q_ready, 8 * T + 2)
            e.tensor_scalar(q, q_new, CLAMP, -CLAMP, ALU.min, ALU.max).then_inc(q_clipped, 1)
            e.wait_ge(q_clipped, T + 1)
            e.tensor_tensor(x_at(T - 1), x_at(T - 1), q, ALU.add).then_inc(vec, 1)


def top_k(nc, mem, a):
    at = [0]

    def place(*shape):
        n = 1
        for k in shape:
            n *= k
        at[0] += n
        return mem.cut(at[0] - n, list(shape))

    ones, before = place(P), place(P)
    eq, rank, one_row = place(NTILE, D), place(2, D), place(D)
    nmax, rsum, rinv = place(NTILE), place(NTILE), place(NTILE)
    count, bit_value, left = (place(B) for _ in range(3))
    candidate, found, bit, taken, next_bit = (place(B).bitcast(I32) for _ in range(5))
    ones16 = place(P).bitcast(BF16)[:, 0:P]
    unused = [place(D) for _ in range(B)]
    mask = [mem.cut(2 * P + b * TC * D // 2, [TC * D // 2]).bitcast(BF16) for b in range(B)]
    row_count, row_before, offset = place(NTILE), place(NTILE), place(NTILE)
    emb_t = mem.gate[:, 0]
    with ExitStack() as ctx:
        def sem(name):
            return ctx.enter_context(nc.semaphore(name))

        emb_loaded, const, turned, copied, max_ready, exp_ready, inv_ready, soft, prod, adj_ready = (
            sem(n) for n in ("emb_loaded", "topk_const", "x4_turned", "x4_copied", "row_max", "row_exp", "row_inv",
                             "row_soft", "adj_product", "adj_ready"))
        mask_ready, summed, counted, chosen = sem("mask_ready"), sem("summed"), sem("counted"), sem("chosen")
        tie, tie_sum, ranked, picked, masked, stored = (
            sem(n) for n in ("tie", "tie_sum", "ranked", "picked", "masked", "stored"))
        bank = mem.psum[0:4]
        block = ctx.enter_context(nc.Block())
        BITS = 31
        STEPS = BITS + 2

        @block.sync
        def _(e):
            for b in range(B):
                e.dma_start(emb_t[:, b], a["cond"][b:b + 1].broadcast_to((P, D))).then_inc(emb_loaded, 16)
            y = a["out"].rearrange("b (t p) d -> b p t d", p=P)
            for b in range(B):
                e.wait_ge(masked, TC * (b + 1))
                e.dma_start(y[b], mem.tok[:, b * TC:(b + 1) * TC]).then_inc(stored, 16)
            e.wait_ge(stored, 16 * B)

        @block.gpsimd
        def _(e):
            e.memset(ones, 1.0).then_inc(const, 1)
            e.memset(ones16, 1.0).then_inc(const, 1)
            e.memset(before, 1.0).then_inc(const, 1)
            e.wait_ge(const, 3)
            e.affine_select(out=before, in_=before, compare_op=ALU.is_gt, fill=0.0, base=0,
                            pattern=[[1, P]], channel_multiplier=-1).then_inc(const, 1)
            for n in range(NTILE):
                t = n % TC
                e.wait_ge(prod, n + 1)
                diag = mem.acc[:, n, t * P:(t + 1) * P]
                e.affine_select(out=diag, in_=diag, compare_op=ALU.not_equal, fill=-3.0e38, base=0,
                                pattern=[[-1, P]], channel_multiplier=1).then_inc(adj_ready, 1)
            for n in range(NTILE):
                e.wait_ge(picked, n + 1)
                e.tensor_tensor(mem.tok[:, n], mem.tok[:, n], eq[:, n], ALU.add).then_inc(masked, 1)

        @block.tensor
        def _(e):
            for n in range(NTILE):
                b, t = n // TC, n % TC
                if n >= 4:
                    e.wait_ge(copied, n - 3)
                for c in range(DC):
                    last = e.transpose(bank[n % 4][:, c * P:(c + 1) * P], mem.feat[:, c, b, t * P:(t + 1) * P],
                                       mem.ident[:, :])
                last.then_inc(turned, 1)
            e.wait_ge(const, 4)

            def sum_masks(step, first=False):
                for b in range(B):
                    if not first:
                        e.wait_ge(counted, B * (step - 1) + b + 1)
                    e.wait_ge(mask_ready, B * step + b + 1)
                    for t in range(TC):
                        last = e.matmul(mem.psum[b][:, :], ones16, mask[b][:, t * D:(t + 1) * D],
                                        start=(t == 0), stop=(t == TC - 1))
                    last.then_inc(summed, 1)

            sum_masks(0, first=True)
            with e.Fori(1, STEPS) as step:
                sum_masks(step)
            e.wait_ge(tie, TC - 1)
            e.matmul(mem.psum[5][:, 0:NTILE], before, row_count, start=True, stop=False)
            e.matmul(mem.psum[5][:, 0:NTILE], ones, row_before, start=False, stop=True).then_inc(tie_sum, 1)

        @block.scalar
        def _(e):
            e.preload_act_table(ACT.Exp)
            for n in range(NTILE + 1):
                if n < NTILE:
                    e.wait_ge(turned, n + 1)
                    e.activation(mem.tok[:, n], bank[n % 4][:, :], ACT.Copy).then_inc(copied, 1)
                if n >= 1:
                    e.wait_ge(max_ready, n)
                    e.activation(mem.acc[:, n - 1], mem.tok[:, n - 1], ACT.Exp, bias=nmax[:, n - 1:n],
                                 accum_out=rsum[:, n - 1:n]).then_inc(exp_ready, 1)
            with e.Fori(0, STEPS) as step:
                for b in range(B):
                    e.wait_ge(summed, B * step + b + 1)
                    e.activation(unused[b], mem.psum[b][:, :], ACT.Copy, accum_out=count[:, b:b + 1]).then_inc(counted, 1)

        @block.vector
        def _(e):
            e.wait_ge(emb_loaded, 16 * B)

            def weigh(n):
                b = n // TC
                e.wait_ge(exp_ready, n + 1)
                e.reciprocal(rinv[:, n:n + 1], rsum[:, n:n + 1]).then_inc(inv_ready, 1)
                e.wait_ge(inv_ready, n + 1)
                e.tensor_scalar(mem.acc[:, n], mem.acc[:, n], rinv[:, n:n + 1], T ** -0.5, ALU.mult, ALU.mult).then_inc(soft, 1)
                e.wait_ge(soft, n + 1)
                e.scalar_tensor_tensor(out=mem.acc[:, n], in0=emb_t[:, b], scalar=mem.emb_s[:, n:n + 1],
                                       in1=mem.acc[:, n], op0=ALU.mult, op1=ALU.mult).then_inc(prod, 1)

            for n in range(NTILE):
                e.wait_ge(copied, n + 1)
                e.tensor_reduce(nmax[:, n:n + 1], mem.tok[:, n], AX.X, ALU.max, negate=True).then_inc(max_ready, 1)
                if n >= 1:
                    weigh(n - 1)
            weigh(NTILE - 1)
            steps = [0]

            def chain(instruction):
                instruction.then_inc(chosen, 1)
                steps[0] += 1
                e.wait_ge(chosen, steps[0])

            def compare(b, threshold, how):
                flat = mem.acc[:, b * TC:(b + 1) * TC].rearrange("p t d -> p (t d)")
                e.tensor_scalar(mask[b], flat, threshold, None, how).then_inc(mask_ready, 1)

            def compare_candidate(g):
                for b in (2 * g, 2 * g + 1):
                    compare(b, candidate[:, b:b + 1].bitcast(F32), ALU.is_ge)

            e.wait_ge(adj_ready, NTILE)
            for b in range(B):
                compare(b, 0.0, ALU.is_ge)
            chain(e.memset(one_row, 1.0))
            chain(e.memset(bit, 1 << 30))
            chain(e.memset(bit_value, float(1 << 30)))
            e.wait_ge(counted, B)
            chain(e.tensor_scalar(found, count, float(TOPK), -1.0, ALU.is_lt, ALU.mult))
            chain(e.tensor_tensor(candidate, found, bit, ALU.bitwise_xor))
            for g in range(2):
                compare_candidate(g)
            head = steps[0]
            CHAIN = 10
            with e.Fori(1, BITS) as k:
                done = [0]

                def link(instruction):
                    instruction.then_inc(chosen, 1)
                    done[0] += 1

                def need(n):
                    e.wait_ge(chosen, CHAIN * k + (head - CHAIN) + n)

                link(e.tensor_scalar(bit, bit, 1, None, ALU.logical_shift_right))
                need(1)
                for g in range(2):
                    pair = slice(2 * g, 2 * g + 2)
                    link(e.tensor_tensor(next_bit[:, pair], found[:, pair], bit[:, pair], ALU.bitwise_xor))
                for g in range(2):
                    pair = slice(2 * g, 2 * g + 2)
                    e.wait_ge(counted, B * k + 2 * g + 2)
                    link(e.scalar_tensor_tensor(out=taken[:, pair], in0=count[:, pair], scalar=float(TOPK),
                                                in1=bit_value[:, pair], op0=ALU.is_ge, op1=ALU.mult))
                    need(done[0])
                    link(e.tensor_tensor(candidate[:, pair], next_bit[:, pair], taken[:, pair], ALU.bitwise_xor))
                    link(e.tensor_tensor(found[:, pair], found[:, pair], taken[:, pair], ALU.bitwise_xor))
                    if g == 1:
                        link(e.tensor_scalar(bit_value, bit_value, 0.5, None, ALU.mult))
                        need(done[0])
                    else:
                        need(done[0] - 1)
                    compare_candidate(g)
                assert done[0] == CHAIN
            steps[0] = head + CHAIN * (BITS - 1)
            e.wait_ge(counted, B * (BITS + 1))
            chain(e.scalar_tensor_tensor(out=taken, in0=count, scalar=float(TOPK), in1=bit_value,
                                         op0=ALU.is_ge, op1=ALU.mult))
            chain(e.tensor_tensor(found, found, taken, ALU.bitwise_xor))
            threshold = found.bitcast(F32)
            for b in range(B):
                compare(b, threshold[:, b:b + 1], ALU.is_gt)
            e.wait_ge(counted, B * STEPS)
            chain(e.tensor_scalar(left, count, -1.0, float(TOPK), ALU.mult, ALU.add))
            for n in range(NTILE):
                b = n // TC
                last = e.tensor_scalar(eq[:, n], mem.acc[:, n], threshold[:, b:b + 1], None, ALU.is_equal, ALU.add,
                                       accum_out=row_count[:, n:n + 1])
            chain(last)
            rows, sums = (r.rearrange("p (b t) -> p t b", b=B) for r in (row_count, row_before))
            chain(e.memset(sums[:, 0], 0.0))
            for t in range(1, TC):
                e.tensor_tensor(sums[:, t], sums[:, t - 1], rows[:, t - 1], ALU.add).then_inc(tie, 1)
                e.wait_ge(tie, t)
            e.wait_ge(tie_sum, 1)
            chain(e.tensor_copy(offset, mem.psum[5][:, 0:NTILE]))
            for n in range(NTILE):
                b = n // TC
                e.tensor_tensor_scan(rank[:, n % 2], one_row, eq[:, n], offset[:, n:n + 1], ALU.mult, ALU.add).then_inc(ranked, 1)
                e.wait_ge(ranked, 2 * n + 1)
                e.scalar_tensor_tensor(out=eq[:, n], in0=rank[:, n % 2], scalar=left[:, b:b + 1], in1=eq[:, n],
                                       op0=ALU.is_le, op1=ALU.mult).then_inc(ranked, 1)
                e.wait_ge(ranked, 2 * n + 2)
                e.scalar_tensor_tensor(out=eq[:, n], in0=mem.acc[:, n], scalar=threshold[:, b:b + 1], in1=eq[:, n],
                                       op0=ALU.is_gt, op1=ALU.add).then_inc(picked, 1)


INPUTS = {"x": "x", "cond": "cond_2048", "fside": "fside_BxSx1_0", "ada_w": "L0_cond_ada_w", "ada_b": "L0_cond_ada_b",
          "qkv_w": "L0_cond_qkv_w", "qkv_b": "L0_cond_qkv_b", "out_w": "L0_cond_out_w", "out_b": "L0_cond_out_b",
          "ffn_w1": "L0_cond_ffn_w1", "ffn_b1": "L0_cond_ffn_b1", "ffn_w2": "L0_cond_ffn_w2", "ffn_b2": "L0_cond_ffn_b2",
          "conv_b": "L1_cond_b", "coupling": "L2_cond_coupling", "bias": "L2_cond_bias"}


def program(nc, a):
    with ExitStack() as ctx:
        mem = Memory(nc, ctx)
        prepare(nc, mem, a)
        attention(nc, mem, a)
        feed_forward(nc, mem, a)
        convolution(nc, mem, a)
        coupled_scan(nc, mem, a)
        top_k(nc, mem, a)


def kernel(**inputs):
    import numpy as np
    import concourse.bacc as bacc
    from concourse.bass_utils import run_bass_kernel_spmd

    nc = bacc.Bacc("TRN2", target_bir_lowering=False, num_devices=1)
    arrays, a = {}, {}
    for short, name in INPUTS.items():
        v = np.ascontiguousarray(inputs[name])
        arrays["in_" + name] = v
        a[short] = nc.dram_tensor("in_" + name, v.shape, mybir.dt.from_np(v.dtype), kind="ExternalInput").ap()
    a["out"] = nc.dram_tensor("out", (B, T, D), F32, kind="ExternalOutput").ap()
    program(nc, a)
    r = run_bass_kernel_spmd(nc, [arrays], core_ids=[0])
    return r.results[0]["out"]
```
